# Optimizing a Trainium2 kernel written in Bass

```python
import numpy as np
import jax
import jax.numpy as jnp

def _softmax(x, axis=-1):
    return jax.nn.softmax(x, axis=axis)

def _gelu(x):
    return jax.nn.gelu(x, approximate=True)

def _silu(x):
    return jax.nn.silu(x)

def _sigmoid(x):
    return jax.nn.sigmoid(x)

def _layernorm(x, axis=-1, eps=1e-05):
    m = jnp.mean(x, axis=axis, keepdims=True)
    v = jnp.var(x, axis=axis, keepdims=True)
    return (x - m) / jnp.sqrt(v + eps)

def _scatter_add(tgt, idx, src, axis=0):
    return tgt.at[idx].add(src)

def _segment_sum(src, seg, n):
    return jax.ops.segment_sum(src, seg, n)
kernel_name = 'mk_adaln_ffn_d2_seqx_r8_d0916f'

def setup_inputs(seed: int=0):
    np.random.seed(seed)
    _w = jnp.asarray

    def _rec_inputs():
        import jax
        import jax.numpy as jnp
        _rk = jax.random.key(seed)
        x = -0.000125 + 0.9999 * jax.random.normal(jax.random.fold_in(_rk, 1), (32, 32, 512), jnp.float32)
        _lenS = 32 - jax.random.randint(jax.random.fold_in(_rk, 7), (32,), 0, max(1, 32 // 4) + 1, jnp.int32)
        _lenS2 = 32 - jax.random.randint(jax.random.fold_in(_rk, 8), (32,), 0, max(1, 32 // 4) + 1, jnp.int32)
        cond_128 = 0.0061147 + 1.02565 * jax.random.normal(jax.random.fold_in(_rk, 11), (32, 128), jnp.float32)
        fside_S_0 = -0.022604 + 0.987366 * jax.random.normal(jax.random.fold_in(_rk, 12), (32,), jnp.float32)
        return (x, cond_128, fside_S_0)
    x, cond_128, fside_S_0 = _rec_inputs()

    def _L0_cond_setup():
        import jax, jax.numpy as jnp
        import numpy as np
        from jax import lax
        N, C_IN, L = (32, 32, 512)
        C_OUT, K, GROUPS = (32, 9, 4)
        C_DIM, PAD, STRIDE = (128, 4, 1)
        key = jax.random.key(seed)
        k1, k2, k3, k4, k5 = jax.random.split(key, 5)
        x = jax.random.normal(k1, (N, C_IN, L), dtype=jnp.float32)
        c = jax.random.normal(k2, (N, C_DIM), dtype=jnp.float32)
        weight = jax.random.normal(k3, (C_OUT, C_IN // GROUPS, K), dtype=jnp.float32)
        c_weight = jax.random.normal(k4, (C_OUT, C_DIM), dtype=jnp.float32)
        bias = jax.random.normal(k5, (C_OUT,), dtype=jnp.float32)
        return {'x': x, 'c': c, 'weight': weight, 'c_weight': c_weight, 'bias': bias}
    _L0_cond_all = _L0_cond_setup()
    _L0_cond_in = {k: v for k, v in _L0_cond_all.items() if k in ('weight', 'c_weight')}
    del _L0_cond_all

    def _L0_ffn_setup():
        import jax, jax.numpy as jnp
        import numpy as np
        HID, INT, LAT, NE, K = (512, 1024, 256, 8, 2)
        LN_EPS = 1e-05

        def _layernorm(x, gamma, beta):
            mu = jnp.mean(x, axis=-1, keepdims=True)
            var = jnp.var(x, axis=-1, keepdims=True)
            return (x - mu) * jax.lax.rsqrt(var + LN_EPS) * gamma + beta
        key = jax.random.key(seed)
        ks = jax.random.split(key, 8)
        s = lambda d: 1.0 / np.sqrt(d)
        return {'hidden_states': jax.random.normal(ks[0], (4, 256, HID), jnp.float32), 'gate_w': jax.random.normal(ks[1], (HID, NE), jnp.float32) * s(HID), 'up_w': jax.random.normal(ks[2], (HID, INT), jnp.float32) * s(HID), 'down_w': jax.random.normal(ks[3], (INT, HID), jnp.float32) * s(INT), 'fc1_w': jax.random.normal(ks[4], (HID, LAT), jnp.float32) * s(HID), 'fc2_w': jax.random.normal(ks[5], (LAT, HID), jnp.float32) * s(LAT), 'expert_w': jax.random.normal(ks[6], (LAT, LAT), jnp.float32), 'ln_gamma': jnp.ones((HID,), jnp.float32), 'ln_beta': jnp.zeros((HID,), jnp.float32)}
    _L0_ffn_all = _L0_ffn_setup()
    _L0_ffn_in = {k: v for k, v in _L0_ffn_all.items() if k in ('gate_w', 'up_w', 'down_w', 'fc1_w', 'fc2_w', 'expert_w', 'ln_gamma', 'ln_beta')}
    del _L0_ffn_all

    def _L1_cond_setup():
        import jax, jax.numpy as jnp
        import numpy as np
        K = 8
        T = 1.0
        D_EMBD = 128
        IN_C = 32
        OUT_C = 32
        BS = 32
        H = 512
        HID = 128
        key = jax.random.key(seed)
        ks = jax.random.split(key, 10)
        s = lambda fan_in: 1.0 / np.sqrt(fan_in)
        return {'x': jax.random.normal(ks[0], (BS, IN_C, H), dtype=jnp.float32), 'embedding': jax.random.normal(ks[1], (BS, D_EMBD), dtype=jnp.float32), 'W0': jax.random.normal(ks[2], (D_EMBD, HID), dtype=jnp.float32) * s(D_EMBD), 'b0': jnp.zeros((HID,), dtype=jnp.float32), 'W1': jax.random.normal(ks[3], (HID, HID), dtype=jnp.float32) * s(HID), 'b1': jnp.zeros((HID,), dtype=jnp.float32), 'W2': jax.random.normal(ks[4], (HID, K), dtype=jnp.float32) * s(HID), 'b2': jnp.zeros((K,), dtype=jnp.float32), 'weight': jax.random.normal(ks[5], (K, OUT_C, IN_C, 1), dtype=jnp.float32) * s(IN_C), 'bias_k': jax.random.normal(ks[6], (K, OUT_C), dtype=jnp.float32) * 0.1}
    _L1_cond_all = _L1_cond_setup()
    _L1_cond_in = {k: v for k, v in _L1_cond_all.items() if k in ('W0', 'b0', 'W1', 'b1', 'W2', 'b2', 'weight', 'bias_k')}
    del _L1_cond_all

    def _L1_ffn_setup():
        import jax, jax.numpy as jnp
        import numpy as np
        import math
        E, DK, R = (8, 32, 16)
        SCALING = 16.0 / 16.0
        key = jax.random.key(seed)
        ks = jax.random.split(key, 7)
        Bt, S, Din, Dout = (4, 256, 512, 512)
        x = jax.random.normal(ks[0], (Bt, S, Din), jnp.float32)
        W = jax.random.normal(ks[1], (Dout, Din), jnp.float32) * 0.02
        b = jnp.zeros((Dout,), jnp.float32)
        Wq = jax.random.normal(ks[2], (E * DK, Din), jnp.float32) * 0.02
        Wk = jax.random.normal(ks[3], (E * DK, Din), jnp.float32) * 0.02
        A = jax.random.normal(ks[4], (E, R, Din), jnp.float32) * 0.02
        Bm = jax.random.normal(ks[5], (E, Dout, R), jnp.float32) * 0.02
        return {'x': x, 'W': W, 'b': b, 'Wq': Wq, 'Wk': Wk, 'A': A, 'Bm': Bm}
    _L1_ffn_all = _L1_ffn_setup()
    _L1_ffn_in = {k: v for k, v in _L1_ffn_all.items() if k in ('W', 'b', 'Wq', 'Wk', 'A', 'Bm')}
    del _L1_ffn_all
    return {'x': x, 'cond_128': cond_128, 'fside_S_0': fside_S_0, 'L0_cond_weight': _L0_cond_in['weight'], 'L0_cond_c_weight': _L0_cond_in['c_weight'], 'L0_ffn_gate_w': _L0_ffn_in['gate_w'], 'L0_ffn_up_w': _L0_ffn_in['up_w'], 'L0_ffn_down_w': _L0_ffn_in['down_w'], 'L0_ffn_fc1_w': _L0_ffn_in['fc1_w'], 'L0_ffn_fc2_w': _L0_ffn_in['fc2_w'], 'L0_ffn_expert_w': _L0_ffn_in['expert_w'], 'L0_ffn_ln_gamma': _L0_ffn_in['ln_gamma'], 'L0_ffn_ln_beta': _L0_ffn_in['ln_beta'], 'L1_cond_W0': _L1_cond_in['W0'], 'L1_cond_b0': _L1_cond_in['b0'], 'L1_cond_W1': _L1_cond_in['W1'], 'L1_cond_b1': _L1_cond_in['b1'], 'L1_cond_W2': _L1_cond_in['W2'], 'L1_cond_b2': _L1_cond_in['b2'], 'L1_cond_weight': _L1_cond_in['weight'], 'L1_cond_bias_k': _L1_cond_in['bias_k'], 'L1_ffn_W': _L1_ffn_in['W'], 'L1_ffn_b': _L1_ffn_in['b'], 'L1_ffn_Wq': _L1_ffn_in['Wq'], 'L1_ffn_Wk': _L1_ffn_in['Wk'], 'L1_ffn_A': _L1_ffn_in['A'], 'L1_ffn_Bm': _L1_ffn_in['Bm']}

def reference(x, cond_128, fside_S_0, L0_cond_weight, L0_cond_c_weight, L0_ffn_gate_w, L0_ffn_up_w, L0_ffn_down_w, L0_ffn_fc1_w, L0_ffn_fc2_w, L0_ffn_expert_w, L0_ffn_ln_gamma, L0_ffn_ln_beta, L1_cond_W0, L1_cond_b0, L1_cond_W1, L1_cond_b1, L1_cond_W2, L1_cond_b2, L1_cond_weight, L1_cond_bias_k, L1_ffn_W, L1_ffn_b, L1_ffn_Wq, L1_ffn_Wk, L1_ffn_A, L1_ffn_Bm):
    import jax
    import jax.numpy as jnp

    def _L0_cond_ref(x, c, weight, c_weight, bias):
        import jax, jax.numpy as jnp
        import numpy as np
        from jax import lax
        N, C_IN, L = (32, 32, 512)
        C_OUT, K, GROUPS = (32, 9, 4)
        C_DIM, PAD, STRIDE = (128, 4, 1)
        out = lax.conv_general_dilated(x, weight, window_strides=(STRIDE,), padding=[(PAD, PAD)], dimension_numbers=('NCH', 'OIH', 'NCH'), feature_group_count=GROUPS)
        ctx = jnp.einsum('nd,od->no', c, c_weight)
        out = out + ctx[:, :, None] + bias[None, :, None]
        return out

    def _L0_ffn_ref(hidden_states, gate_w, up_w, down_w, fc1_w, fc2_w, expert_w, ln_gamma, ln_beta):
        import jax, jax.numpy as jnp
        import numpy as np
        HID, INT, LAT, NE, K = (512, 1024, 256, 8, 2)
        LN_EPS = 1e-05

        def _layernorm(x, gamma, beta):
            mu = jnp.mean(x, axis=-1, keepdims=True)
            var = jnp.var(x, axis=-1, keepdims=True)
            return (x - mu) * jax.lax.rsqrt(var + LN_EPS) * gamma + beta
        logits = jnp.einsum('bsh,he->bse', hidden_states, gate_w)
        routing_weights, selected_experts = jax.lax.top_k(logits, K)
        h = jax.nn.relu(jnp.einsum('bsh,hi->bsi', hidden_states, up_w)) ** 2
        shared_out = jnp.einsum('bsi,ih->bsh', h, down_w)
        x_latent = jnp.einsum('bsh,hl->bsl', hidden_states, fc1_w)
        expert_out = jnp.einsum('bsl,lm->bsm', x_latent, expert_w)
        moe_out = expert_out * jnp.sum(routing_weights, axis=-1, keepdims=True)
        routed_out = jnp.einsum('bsl,lh->bsh', moe_out, fc2_w)
        return _layernorm(shared_out + routed_out, ln_gamma, ln_beta)

    def _L1_cond_ref(x, embedding, W0, b0, W1, b1, W2, b2, weight, bias_k):
        import jax, jax.numpy as jnp
        import numpy as np
        K = 8
        T = 1.0
        D_EMBD = 128
        IN_C = 32
        OUT_C = 32
        BS = 32
        H = 512
        HID = 128
        h = jax.nn.gelu(embedding @ W0 + b0, approximate=False)
        h = jax.nn.gelu(h @ W1 + b1, approximate=False)
        att = jax.nn.softmax((h @ W2 + b2) / T, axis=-1)
        agg_w = jnp.einsum('bk,koi->boi', att, weight[..., 0])
        agg_b = att @ bias_k
        out = jnp.einsum('boi,bih->boh', agg_w, x) + agg_b[:, :, None]
        return out

    def _L1_ffn_ref(x, W, b, Wq, Wk, A, Bm):
        import jax, jax.numpy as jnp
        import numpy as np
        import math
        E, DK, R = (8, 32, 16)
        SCALING = 16.0 / 16.0
        Bt, S, Din = x.shape
        result = jnp.einsum('bsi,oi->bso', x, W) + b
        q = jnp.einsum('bsi,ni->bsn', x, Wq).reshape(Bt, S, E, DK)
        k = jnp.einsum('bsi,ni->bsn', x, Wk).reshape(Bt, S, E, DK)
        scores = jnp.einsum('bsed,bsed->bse', q, k) / math.sqrt(DK)
        w = jax.nn.softmax(scores, axis=-1)
        h = jnp.einsum('bsi,eri->bser', x, A)
        combined = jnp.einsum('bse,bser,eor->bso', w, h, Bm) * SCALING
        return result + combined
    x = x + _L0_ffn_ref(_L0_cond_ref(x, cond_128, L0_cond_weight, L0_cond_c_weight, fside_S_0), L0_ffn_gate_w, L0_ffn_up_w, L0_ffn_down_w, L0_ffn_fc1_w, L0_ffn_fc2_w, L0_ffn_expert_w, L0_ffn_ln_gamma, L0_ffn_ln_beta)
    x = x + _L1_ffn_ref(_L1_cond_ref(x, cond_128, L1_cond_W0, L1_cond_b0, L1_cond_W1, L1_cond_b1, L1_cond_W2, L1_cond_b2, L1_cond_weight, L1_cond_bias_k), L1_ffn_W, L1_ffn_b, L1_ffn_Wq, L1_ffn_Wk, L1_ffn_A, L1_ffn_Bm)
    return x

_drawn_inputs = setup_inputs


def setup_inputs(seed=0):
    import zlib

    import numpy as np

    out = dict(_drawn_inputs(seed))
    spreads = {'L0_ffn_ln_gamma': (1.0, 0.2),
     'L0_ffn_ln_beta': (0.0, 0.1),
     'L1_cond_b0': (0.0, 0.8),
     'L1_cond_b1': (0.0, 0.8),
     'L1_cond_b2': (0.0, 0.623),
     'L1_ffn_b': (0.0, 0.1)}
    factors = {'L1_cond_bias_k': 5.069,
     'L1_ffn_Wq': 8.0,
     'L1_ffn_Wk': 8.0,
     'L1_ffn_A': 8.0,
     'L1_ffn_Bm': 8.0}
    for name, (base, spread) in spreads.items():
        noise = np.random.default_rng([zlib.crc32(name.encode()), seed]).standard_normal(out[name].shape)
        drawn = base * np.exp(spread * noise) if base else spread * noise
        out[name] = jnp.asarray(drawn.astype(out[name].dtype))
    for name, factor in factors.items():
        out[name] = (out[name] * factor).astype(out[name].dtype)
    return out
```

```python
import math
from contextlib import ExitStack

import concourse.bass as bass
from concourse import mybir

F32 = mybir.dt.float32
F32R = mybir.dt.float32r
ALU = mybir.AluOpType
ACT = mybir.ActivationFunctionType
AX_X = mybir.AxisListType.X

P = 128
BANK = 512


def bass_adaln_ffn(
    nc: bass.Bass,
    x: bass.AP,
    cond_128: bass.AP,
    fside_S_0: bass.AP,
    L0_cond_weight: bass.AP,
    L0_cond_c_weight: bass.AP,
    L0_ffn_gate_w: bass.AP,
    L0_ffn_up_w: bass.AP,
    L0_ffn_down_w: bass.AP,
    L0_ffn_fc1_w: bass.AP,
    L0_ffn_fc2_w: bass.AP,
    L0_ffn_expert_w: bass.AP,
    L0_ffn_ln_gamma: bass.AP,
    L0_ffn_ln_beta: bass.AP,
    L1_cond_W0: bass.AP,
    L1_cond_b0: bass.AP,
    L1_cond_W1: bass.AP,
    L1_cond_b1: bass.AP,
    L1_cond_W2: bass.AP,
    L1_cond_b2: bass.AP,
    L1_cond_weight: bass.AP,
    L1_cond_bias_k: bass.AP,
    L1_ffn_W: bass.AP,
    L1_ffn_b: bass.AP,
    L1_ffn_Wq: bass.AP,
    L1_ffn_Wk: bass.AP,
    L1_ffn_A: bass.AP,
    L1_ffn_Bm: bass.AP,
    out: bass.AP,
):
    N, C, L = x.shape
    CD = cond_128.shape[1]
    INT = L0_ffn_up_w.shape[1]
    LAT = L0_ffn_fc1_w.shape[1]
    NE = L0_ffn_gate_w.shape[1]
    KT = L0_cond_weight.shape[2]
    CG = L0_cond_weight.shape[1]
    KE, CHID = L1_cond_W2.shape[1], L1_cond_W0.shape[1]
    E, R, _ = L1_ffn_A.shape
    DK = L1_ffn_Wq.shape[0] // E
    EPS = 1e-5

    SPT = P // C
    TILES = N // SPT
    HALVES = 2
    TPH = TILES // HALVES
    NPH = N // HALVES
    TOKH = TPH * P
    PH = L // P
    IC = INT // P
    LC = LAT // P
    G = C // CG
    QW = E * DK
    HH = E * R // 2
    EH = E // 2
    QKW = QW + HH
    NWIN = 3
    PADK = KT // 2
    XW = P + 2
    SCALE = 1.0 / math.sqrt(DK)
    assert L == BANK and TOKH == BANK and PH == 4 and C == 32 and KT == 9 and 2 * QKW == 640
    NR = 3

    xt_dram = x.rearrange("(t s) c l -> (s c) t l", s=SPT)
    out_dram = out.rearrange("(t s) c l -> (s c) t l", s=SPT)

    with ExitStack() as ctx:
        def sb(name, shape, dt=F32, scope=ctx):
            return scope.enter_context(nc.sbuf_tensor(name, shape, dt))

        def sem(name):
            return ctx.enter_context(nc.semaphore(name))

        PS = ctx.enter_context(nc.psum_tensor("PS", [P, 8, BANK], F32))
        D = [PS[:, b, :] for b in range(4)]
        U = [PS[:, 4, :], PS[:, 5, :]]
        M = [PS[:, 6, :], PS[:, 7, :]]
        QK = [(U[0], U[1]), (M[0], M[1])]

        ident = sb("ident", [P, P])
        ones = sb("ones", [P, P])
        X = sb("X", [P, TILES, L])
        XS = sb("XS", [P, NPH, XW])
        wconv = sb("wconv", [P, NWIN, P])
        up_hi = sb("up_hi", [P, IC, PH, P], F32R)
        up_lo = sb("up_lo", [P, IC, PH, P], F32R)
        dn_hi = sb("dn_hi", [P, IC, L], F32R)
        dn_lo = sb("dn_lo", [P, IC, L], F32R)
        fc_hi = sb("fc_hi", [P, PH, LAT], F32R)
        fc_lo = sb("fc_lo", [P, PH, LAT], F32R)
        ex_hi = sb("ex_hi", [P, LC, L], F32R)
        ex_lo = sb("ex_lo", [P, LC, L], F32R)
        gate = sb("gate", [P, PH, NE])
        gamma = sb("gamma", [P, L])
        rowb = sb("rowb", [P, L])
        B0 = sb("B0", [P, N * C])
        B1 = sb("B1", [P, N * C])
        BD = sb("BD", [P, TILES, P])
        H_hi = sb("H_hi", [P, PH, TOKH], F32R)
        H_lo = sb("H_lo", [P, PH, TOKH], F32R)
        tf = sb("tf", [P, 2, PH, P])
        sbc = sb("sbc", [P, TOKH])
        top = sb("top", [P, 2, 8])
        ssum = sb("ssum", [P, TPH])
        st6 = sb("st6", [P, 2, 6])
        mv = sb("mv", [P, TPH, 2])
        ve = sb("ve", [P, TPH])
        nhalf = sb("nhalf", [P, 1])
        rstd = sb("rstd", [P, TPH])
        qk_raw = sb("qk_raw", [P, 2, LC, L])
        qs = sb("qs", [P, QW])
        pr = sb("pr", [P, QW])
        hw = sb("hw", [P, P])
        hwT_hi = sb("hwT_hi", [P, 2, P], F32R)
        hwT_lo = sb("hwT_lo", [P, 2, P], F32R)
        sm = sb("sm", [P, 2, 4, E])

        with ExitStack() as early:
            def se(name, shape):
                return sb(name, shape, F32, early)
            c_nat = se("c_nat", [N, CD])
            cw_nat = se("cw_nat", [C, CD])
            cT = se("cT", [CD, N])
            prod0 = se("prod0", [CD, N, C])
            fside = se("fside", [1, C])
            wc_nat = se("wc_nat", [C, CG, KT])
            WKW = 15
            wc_pad = se("wc_pad", [P, CG, WKW])
            blk = se("blk", [P, SPT, G])
            gmask = se("gmask", [P, G])
            exraw = se("exraw", [P, LC, LAT])
            exT = se("exT", [P, LC, LAT])
            W0 = se("W0", [CD, CHID])
            W1 = se("W1", [CHID, CHID])
            W2 = se("W2", [CHID, KE])
            b0 = se("b0", [CHID, 1])
            b1 = se("b1", [CHID, 1])
            b2 = se("b2", [N, KE])
            h1 = se("h1", [CHID, N])
            h2 = se("h2", [CHID, N])
            att = se("att", [N, 4, KE])
            attT = se("attT", [KE, N])
            wk = se("wk", [KE, C, C])
            bk = se("bk", [KE, C])
            prod1 = se("prod1", [KE, N, C])
        relu = sb("relu", [P, TOKH])
        R_hi = sb("R_hi", [P, NR, TOKH], F32R)
        R_lo = sb("R_lo", [P, NR, TOKH], F32R)
        lat_hi = sb("lat_hi", [P, LC, TOKH], F32R)
        lat_lo = sb("lat_lo", [P, LC, TOKH], F32R)

        with ExitStack() as raw:
            up_raw = sb("up_raw", [P, PH, INT], F32, raw)
            dn_raw = sb("dn_raw", [P, IC, L], F32, raw)
            fc_raw = sb("fc_raw", [P, PH, LAT], F32, raw)
            fc2 = sb("fc2", [P, LC, L], F32, raw)
        wT_hi = sb("wT_hi", [P, PH, L], F32R)
        wT_lo = sb("wT_lo", [P, PH, L], F32R)
        qkT_hi = sb("qkT_hi", [P, PH, 2, QKW], F32R)
        qkT_lo = sb("qkT_lo", [P, PH, 2, QKW], F32R)
        bT_hi = sb("bT_hi", [P, L], F32R)
        bT_lo = sb("bT_lo", [P, L], F32R)

        w_raw = XS[:].rearrange("p n w -> p (n w)")[:, 0:PH * L].rearrange("p (c l) -> p c l", c=PH)
        tflat = tf[:].rearrange("p a b c -> p (a b c)")
        a_raw = tflat[:, 0:L]
        b_raw = tflat[:, L:2 * L].rearrange("p (c e r) -> p c e r", c=PH, e=E)

        ld_c = sem("ld_c")
        ld_wc = sem("ld_wc")
        ld_x = [sem(f"ld_x{i}") for i in range(TILES // 2)]
        ld_ex = sem("ld_ex")
        ld_fc2 = sem("ld_fc2")
        ld_up = [sem(f"ld_up{i}") for i in range(2)]
        ld_fc = sem("ld_fc")
        ld_gate = sem("ld_gate")
        ld_dn = [sem(f"ld_dn{i}") for i in range(2)]
        ld_cond = sem("ld_cond")
        ld_gb = sem("ld_gb")
        ld_b = sem("ld_b")
        ld_w = sem("ld_w")
        ld_qk = sem("ld_qk")
        ld_ab = sem("ld_ab")
        s_ones = sem("s_ones")
        s_ident = sem("s_ident")
        s_blk = sem("s_blk")
        s_zero = sem("s_zero")
        s_gmask = sem("s_gmask")
        s_cTp = sem("s_cTp")
        s_cT = sem("s_cT")
        s_prod0 = sem("s_prod0")
        s_wcp = sem("s_wcp")
        s_wconv = sem("s_wconv")
        s_B0p = sem("s_B0p")
        s_B0 = sem("s_B0")
        s_exTp = sem("s_exTp")
        s_exT = sem("s_exT")
        s_E2p = sem("s_E2p")
        s_E2h = sem("s_E2h")
        s_E2 = sem("s_E2")
        s_c1p = sem("s_c1p")
        s_c1 = sem("s_c1")
        s_c2p = sem("s_c2p")
        s_c2 = sem("s_c2")
        s_lgp = sem("s_lgp")
        s_att = sem("s_att")
        s_aexp = sem("s_aexp")
        s_aTp = sem("s_aTp")
        s_aT = sem("s_aT")
        s_prod1 = sem("s_prod1")
        s_AGp = sem("s_AGp")
        s_BD = sem("s_BD")
        s_B1p = sem("s_B1p")
        s_B1 = sem("s_B1")
        s_uph = sem("s_uph")
        s_up = sem("s_up")
        s_fch = sem("s_fch")
        s_fc = sem("s_fc")
        s_dnh = sem("s_dnh")
        s_dn = sem("s_dn")
        s_wgp = sem("s_wgp")
        s_wgh = sem("s_wgh")
        s_wg = sem("s_wg")
        xs_v = sem("xs_v")
        xs_a = sem("xs_a")
        s_conv = sem("s_conv")
        s_tf = sem("s_tf")
        s_Hh = sem("s_Hh")
        s_H = sem("s_H")
        s_gp = sem("s_gp")
        s_top = sem("s_top")
        s_sum = sem("s_sum")
        s_diag = sem("s_diag")
        s_sbp = sem("s_sbp")
        s_sb = sem("s_sb")
        s_latp = sem("s_latp")
        s_lats = sem("s_lats")
        s_lath = sem("s_lath")
        s_lat = sem("s_lat")
        s_upp = sem("s_upp")
        s_relu = sem("s_relu")
        s_sq = sem("s_sq")
        s_Rh = sem("s_Rh")
        s_R = sem("s_R")
        s_down = sem("s_down")
        s_ffn = sem("s_ffn")
        s_bn = sem("s_bn")
        s_mv = sem("s_mv")
        s_ve = sem("s_ve")
        s_rstd = sem("s_rstd")
        s_cen = sem("s_cen")
        s_x1 = sem("s_x1")
        s_xb = sem("s_xb")
        s_yp = sem("s_yp")
        s_yb = sem("s_yb")
        s_Yh = sem("s_Yh")
        s_Y = sem("s_Y")
        s_x1b = sem("s_x1b")
        s_qkp = sem("s_qkp")
        s_q = sem("s_q")
        s_pr = sem("s_pr")
        s_sc = sem("s_sc")
        s_mx = sem("s_mx")
        s_nmx = sem("s_nmx")
        s_e = sem("s_e")
        s_rc = sem("s_rc")
        s_hw = sem("s_hw")
        s_hwp = sem("s_hwp")
        s_hwh = sem("s_hwh")
        s_hwT = sem("s_hwT")
        s_res = sem("s_res")
        s_fin = sem("s_fin")
        s_out = sem("s_out")

        block = ctx.enter_context(nc.Block())

        wgroups = [("w", p) for p in range(PH)] + [("a", 0), ("b", 0)] + [("qk", p) for p in range(PH)]

        def wg_dst(g, hi):
            what, p = wgroups[g]
            if what == "w":
                return [((wT_hi if hi else wT_lo)[:, p, :], M[g % 2])]
            if what == "b":
                return [((bT_hi if hi else bT_lo)[:], M[g % 2])]
            t = qkT_hi if hi else qkT_lo
            if what == "qk":
                return [(t[:, p, :, 0:QW], M[g % 2].rearrange("p (a q) -> p a q", a=2))]
            return [(t[:, :, a, QW:QKW],
                     M[g % 2].rearrange("p (c a q) -> p a c q", c=PH, a=2)[:, a]) for a in range(2)]

        def bcast_mid(ap, n):
            return ap.unsqueeze(1).broadcast_to([ap.shape[0], n, *ap.shape[1:]])

        def down_done(eng, i):
            h, c = divmod(i, IC)
            if c == IC - 1:
                eng.wait_ge(s_ffn, TPH * (h + 1))
            else:
                eng.wait_ge(s_down, h * (IC - 1) + c + 1)

        def phase_copy(eng, s, j, t0, t1):
            src = X[C * s:C * (s + 1), t0:t1, :].rearrange("p t (m j) -> p t m j", j=PH)[:, :, :, j]
            a, b = t0 % TPH, (t1 - 1) % TPH + 1
            dst = XS[C * j:C * (j + 1), a * SPT:b * SPT, 1:1 + P]\
                .rearrange("p (t s) m -> p t s m", s=SPT)[:, :, s]
            if eng is nc.vector:
                return nc.vector.tensor_copy(dst, src)
            return nc.scalar.activation(dst, src, ACT.Copy)

        @block.sync
        def _(sp):
            for i in range(TPH // 2):
                sp.dma_start(X[:, 2 * i:2 * i + 2, :], xt_dram[:, 2 * i:2 * i + 2, :]).then_inc(ld_x[i], 16)
            sp.dma_start(exraw[:], L0_ffn_expert_w.rearrange("(c p) m -> p c m", p=P)).then_inc(ld_ex, 16)
            upv = L0_ffn_up_w.rearrange("(m p) i -> m p i", p=PH)
            sp.dma_start(up_raw[:, :, 0:INT // 2], upv[:, :, 0:INT // 2]).then_inc(ld_up[0], 16)
            sp.dma_start(fc2[:], L0_ffn_fc2_w.rearrange("(c p) l -> p c l", p=P)).then_inc(ld_fc2, 16)
            sp.dma_start(up_raw[:, :, INT // 2:INT], upv[:, :, INT // 2:INT]).then_inc(ld_up[1], 16)
            sp.dma_start(fc_raw[:], L0_ffn_fc1_w.rearrange("(m p) i -> m p i", p=PH)).then_inc(ld_fc, 16)
            dnv = L0_ffn_down_w.rearrange("(c p) l -> p c l", p=P)
            for i in range(2):
                cs = slice(i * IC // 2, (i + 1) * IC // 2)
                sp.dma_start(dn_raw[:, cs, :], dnv[:, cs, :]).then_inc(ld_dn[i], 16)
            for i in range(TPH // 2, TILES // 2):
                sp.dma_start(X[:, 2 * i:2 * i + 2, :], xt_dram[:, 2 * i:2 * i + 2, :]).then_inc(ld_x[i], 16)
            sp.dma_start(gamma[:], L0_ffn_ln_gamma.partition_broadcast(P)).then_inc(ld_gb, 16)
            sp.dma_start(rowb[:], L0_ffn_ln_beta.partition_broadcast(P)).then_inc(ld_gb, 16)
            for i, w in enumerate((L1_ffn_Wq, L1_ffn_Wk)):
                sp.dma_start(qk_raw[:, i], w.rearrange("(c p) l -> p c l", p=P)).then_inc(ld_qk, 16)
            sp.wait_ge(s_conv, TILES)
            sp.dma_start(w_raw, L1_ffn_W.rearrange("(c p) l -> p c l", p=P)).then_inc(ld_w, 16)
            sp.wait_ge(s_gp, TILES)
            sp.wait_ge(s_H, TILES)
            sp.dma_start(a_raw, L1_ffn_A.rearrange("e r l -> (e r) l")).then_inc(ld_ab, 16)
            bv = L1_ffn_Bm.rearrange("e (c p) r -> p c e r", p=P)
            for c in range(PH):
                sp.dma_start(b_raw[:, c], bv[:, c]).then_inc(ld_ab, 16)
            sp.wait_ge(s_xb, TILES)
            sp.dma_start(rowb[:], L1_ffn_b.partition_broadcast(P)).then_inc(ld_b, 16)
            for T in range(TILES):
                sp.wait_ge(s_fin, T + 1)
                sp.dma_start(out_dram[:, T, :], X[:, T, :]).then_inc(s_out, 16)
            sp.wait_ge(s_out, 16 * TILES)

        @block.gpsimd
        def _(pool):
            nc.gpsimd.memset(ident[:], 0.0).then_inc(s_ident, 1)
            nc.gpsimd.memset(wc_pad[:], 0.0).then_inc(s_zero, 1)
            pool.wait_ge(s_ident, 1)
            nc.gpsimd.affine_select(out=ident[:], in_=ident[:], compare_op=ALU.not_equal, fill=1.0, base=0,
                                    pattern=[[-1, P]], channel_multiplier=1).then_inc(s_ident, 1)
            nc.gpsimd.memset(blk[:], 1.0).then_inc(s_blk, 1)
            pool.wait_ge(s_blk, 1)
            pat = [[-C, SPT], [-CG, G]]
            nc.gpsimd.affine_select(out=blk[:], in_=blk[:], compare_op=ALU.is_ge, fill=0.0, base=0,
                                    pattern=pat, channel_multiplier=1).then_inc(s_blk, 1)
            pool.wait_ge(s_blk, 2)
            nc.gpsimd.affine_select(out=blk[:], in_=blk[:], compare_op=ALU.is_ge, fill=0.0, base=CG - 1,
                                    pattern=[[C, SPT], [CG, G]], channel_multiplier=-1).then_inc(s_blk, 1)
            nc.gpsimd.memset(XS[:, :, 0:1], 0.0)
            nc.gpsimd.memset(XS[:, :, XW - 1:XW], 0.0).then_inc(s_zero, 1)
            nc.gpsimd.memset(nhalf[:], -0.5)
            nc.gpsimd.memset(BD[:], 0.0).then_inc(s_zero, 1)
            pool.wait_ge(s_fch, 1)
            nc.gpsimd.tensor_tensor(fc_lo[:], fc_raw[:], fc_hi[:].bitcast(F32), ALU.subtract).then_inc(s_fc, 1)
            for c in range(IC):
                pool.wait_ge(s_dnh, c + 1)
                nc.gpsimd.tensor_tensor(dn_lo[:, c, :], dn_raw[:, c, :], dn_hi[:, c, :].bitcast(F32),
                                        ALU.subtract).then_inc(s_dn, 1)
            pool.wait_ge(ld_gb, 32)

            def add_beta(h):
                pool.wait_ge(xs_v, (2, 3)[h])
                pool.wait_ge(xs_a, (2, 3)[h])
                for t in range(TPH):
                    T = h * TPH + t
                    nc.gpsimd.tensor_tensor(X[:, T, :], X[:, T, :], rowb[:], ALU.add).then_inc(s_xb, 1)

            def norm_scale(T):
                t = T % TPH
                pool.wait_ge(s_mv, T + 1)
                if T >= TPH:
                    pool.wait_ge(s_x1, T - TPH + 1)
                nc.gpsimd.tensor_scalar(ve[:, t:t + 1], mv[:, t, 1:2], EPS, 1.0, ALU.add, ALU.mult)\
                    .then_inc(s_ve, 1)
                pool.wait_ge(s_ve, T + 1)
                nc.gpsimd.tensor_tensor(rstd[:, t:t + 1], ve[:, t:t + 1], nhalf[:], ALU.pow).then_inc(s_rstd, 1)

            def add_bias(h):
                for t in range(TPH):
                    T = h * TPH + t
                    pool.wait_ge(s_yp, T + 1)
                    nc.gpsimd.tensor_tensor(X[:, T, :], X[:, T, :], rowb[:], ALU.add).then_inc(s_x1b, 1)

            add_beta(0)
            add_beta(1)
            for T in range(TILES):
                norm_scale(T)
            pool.wait_ge(ld_b, 16)
            add_bias(0)
            add_bias(1)

        @block.scalar
        def _(act):
            act.dma_start(c_nat[:], cond_128).then_inc(ld_c, 16)
            act.dma_start(cw_nat[:], L0_cond_c_weight).then_inc(ld_c, 16)
            act.dma_start(fside[:], fside_S_0.rearrange("(a o) -> a o", a=1)).then_inc(ld_c, 16)
            wcv = L0_cond_weight.rearrange("(g o) i k -> g i o k", g=G)
            for g in range(G):
                act.dma_start(wc_nat[CG * g:CG * (g + 1)], wcv[g]).then_inc(ld_wc, 16)
            for dst, src in ((W0, L1_cond_W0), (W1, L1_cond_W1), (W2, L1_cond_W2), (bk, L1_cond_bias_k)):
                act.dma_start(dst[:], src).then_inc(ld_cond, 16)
            for dst, src in ((b0, L1_cond_b0), (b1, L1_cond_b1)):
                act.dma_start(dst[:], src.rearrange("(p a) -> p a", a=1)).then_inc(ld_cond, 16)
            act.dma_start(b2[:], L1_cond_b2.partition_broadcast(N)).then_inc(ld_cond, 16)
            act.dma_start(wk[:], L1_cond_weight.rearrange("k o i a -> k o (i a)")).then_inc(ld_cond, 16)
            act.dma_start(gate[:], L0_ffn_gate_w.rearrange("(m p) e -> m p e", p=PH)).then_inc(ld_gate, 16)

            def shift_copies(t0, t1):
                for j in range(PH):
                    last = phase_copy(nc.scalar, SPT - 1, j, t0, t1)
                last.then_inc(xs_a, 1)

            def split_up(c):
                act.wait_ge(ld_up[c // (IC // 2)], 16)
                nc.scalar.activation(up_hi[:, c], up_raw[:, :, c * P:(c + 1) * P], ACT.Copy).then_inc(s_uph, 1)

            def split_dn(c):
                act.wait_ge(ld_dn[c // (IC // 2)], 16)
                nc.scalar.activation(dn_hi[:, c, :], dn_raw[:, c, :], ACT.Copy).then_inc(s_dnh, 1)

            def split_H(T):
                t = T % TPH
                act.wait_ge(s_tf, T + 1)
                nc.scalar.activation(H_hi[:, :, t * P:(t + 1) * P], tf[:, T % 2], ACT.Copy).then_inc(s_Hh, 1)

            def up_relu(i):
                act.wait_ge(s_upp, i + 1)
                if i:
                    act.wait_ge(s_sq, i)
                nc.scalar.activation(relu[:], U[i % 2], ACT.Relu).then_inc(s_relu, 1)

            def up_split(i):
                act.wait_ge(s_sq, i + 1)
                if i >= NR:
                    down_done(act, i - NR)
                nc.scalar.activation(R_hi[:, i % NR], U[i % 2], ACT.Copy).then_inc(s_Rh, 1)

            def scale_rows(h):
                act.wait_ge(s_sbp, h + 1)
                nc.scalar.activation(sbc[:], M[0], ACT.Copy).then_inc(s_sb, 1)

            def lat_split(n):
                act.wait_ge(s_lats, n + 1)
                nc.scalar.activation(lat_hi[:, n % LC], M[(n + 1) % LC], ACT.Copy).then_inc(s_lath, 1)

            def group_split(g):
                act.wait_ge(s_wgp, g + 1)
                for dst, src in wg_dst(g, True):
                    last = nc.scalar.activation(dst, src, ACT.Copy)
                last.then_inc(s_wgh, 1)

            act.wait_ge(ld_x[0], 16)
            shift_copies(0, 2)
            for i in range(2):
                act.wait_ge(s_B0p, i + 1)
                nc.scalar.activation(B0[:, i * BANK:(i + 1) * BANK], D[i], ACT.Copy).then_inc(s_B0, 1)
            act.wait_ge(ld_x[1], 16)
            shift_copies(2, 4)
            act.wait_ge(ld_cond, 16 * 8)
            act.wait_ge(s_c1p, 1)
            nc.scalar.activation(h1[:], D[0][:, 0:N], ACT.Gelu, bias=b0[:, 0:1]).then_inc(s_c1, 1)
            split_up(0)
            split_H(0)
            act.wait_ge(s_c2p, 1)
            nc.scalar.activation(h2[:], D[1][:, 0:N], ACT.Gelu, bias=b1[:, 0:1]).then_inc(s_c2, 1)
            split_up(1)
            split_H(1)
            act.wait_ge(s_exTp, 1)
            nc.scalar.activation(exT[:].rearrange("p c m -> p (c m)"), D[2], ACT.Copy).then_inc(s_exT, 1)
            act.wait_ge(s_att, 3)
            nc.scalar.activation(att[:, 2, :], att[:, 1, :], ACT.Exp, accum_out=att[:, 3, 0:1]).then_inc(s_aexp, 1)
            split_H(2)
            split_up(2)
            for i in range(LC):
                act.wait_ge(s_E2p, i + 1)
                nc.scalar.activation(ex_hi[:, i, :], (D[3], M[1])[i], ACT.Copy).then_inc(s_E2h, 1)
            split_H(3)
            act.wait_ge(s_aTp, 1)
            nc.scalar.activation(attT[:], D[0][0:KE, 0:N], ACT.Copy).then_inc(s_aT, 1)
            split_up(3)
            act.wait_ge(s_AGp, 1)
            act.wait_ge(s_zero, 3)
            for b in range(2):
                ag = D[b].rearrange("p (o t s) -> p s t o", t=TILES, s=SPT)
                for s in range(SPT):
                    last = nc.scalar.activation(BD[C * s:C * (s + 1), :, C * s + b * (C // 2):C * s + (b + 1) * (C // 2)],
                                                ag[0:C, s], ACT.Copy)
            last.then_inc(s_BD, 1)
            for i in range(2):
                act.wait_ge(s_B1p, i + 1)
                nc.scalar.activation(B1[:, i * BANK:(i + 1) * BANK], D[2 + i], ACT.Copy).then_inc(s_B1, 1)

            for h in range(HALVES):
                if h:
                    for t in range(TPH):
                        split_H(h * TPH + t)
                    for t in range(TPH):
                        pass
                i0 = h * IC
                up_relu(i0)
                up_split(i0)
                if h == 0:
                    act.wait_ge(ld_fc, 16)
                    nc.scalar.activation(fc_hi[:], fc_raw[:], ACT.Copy).then_inc(s_fch, 1)
                    split_up(4)
                up_relu(i0 + 1)
                up_split(i0 + 1)
                scale_rows(h)
                if h == 0:
                    split_dn(0)
                    split_up(5)
                for n in range(LC):
                    lat_split(h * LC + n)
                    if h == 0:
                        split_dn(1 + n)
                        split_up(6 + n)
                for c in range(2, IC):
                    up_relu(i0 + c)
                    up_split(i0 + c)
                    if h == 0:
                        if c + 1 < IC:
                            split_dn(c + 1)
                        if c == 3:
                            act.wait_ge(ld_x[2], 16)
                            act.wait_ge(ld_x[3], 16)
                            act.wait_ge(s_conv, TPH)
                            shift_copies(TPH, TILES)
                    else:
                        group_split(c - 2)
                if h:
                    for g in range(IC - 2, len(wgroups)):
                        group_split(g)

            def y_split(T):
                t = T % TPH
                act.wait_ge(s_yb, T + 1)
                nc.scalar.activation(H_hi[:, :, t * P:(t + 1) * P],
                                     M[T % 2].rearrange("p (c t) -> p c t", c=PH), ACT.Copy).then_inc(s_Yh, 1)

            def q_copy(T):
                act.wait_ge(s_qkp, T + 1)
                if T:
                    act.wait_ge(s_pr, T)
                nc.scalar.activation(qs[:], QK[T % 2][0][:, 0:QW], ACT.Copy).then_inc(s_q, 1)

            def exp_scores(T):
                act.wait_ge(s_nmx, T + 1)
                nc.scalar.activation(sm[:, T % 2, 2, :], sm[:, T % 2, 0, :], ACT.Exp, scale=SCALE,
                                     bias=sm[:, T % 2, 1, 1:2], accum_out=sm[:, T % 2, 3, 0:1]).then_inc(s_e, 1)

            def hw_split(T):
                act.wait_ge(s_hwp, T + 1)
                if T >= 2:
                    act.wait_ge(s_res, T - 1)
                nc.scalar.activation(hwT_hi[:, T % 2], QK[T % 2][0][:, 0:P], ACT.Copy).then_inc(s_hwh, 1)

            for h in range(HALVES):
                for t in range(TPH):
                    y_split(h * TPH + t)
                for t in range(TPH):
                    T = h * TPH + t
                    q_copy(T)
                    exp_scores(T)
                    hw_split(T)

        @block.vector
        def _(dve):
            def shift_copies(t0, t1):
                for s in range(SPT - 1):
                    for j in range(PH):
                        last = phase_copy(nc.vector, s, j, t0, t1)
                last.then_inc(xs_v, 1)

            def split_up(c):
                dve.wait_ge(s_uph, c + 1)
                nc.vector.tensor_tensor(up_lo[:, c], up_raw[:, :, c * P:(c + 1) * P], up_hi[:, c].bitcast(F32),
                                        ALU.subtract).then_inc(s_up, 1)

            def add_ctx(T):
                dve.wait_ge(s_conv, T + 1)
                dve.wait_ge(s_B0, 2)
                if T >= 2:
                    dve.wait_ge(s_gp, T - 1)
                    dve.wait_ge(s_H, T - 1)
                nc.vector.tensor_tensor(
                    tf[:, T % 2].rearrange("m p (n o) -> m n p o", o=C),
                    U[T % 2].rearrange("m (n p o) -> m n p o", n=SPT, p=PH),
                    B0[:, T * P:(T + 1) * P].rearrange("m (n o) -> m n o", o=C).unsqueeze(2)
                    .broadcast_to([P, SPT, PH, C]), ALU.add).then_inc(s_tf, 1)

            def split_H(T):
                t = T % TPH
                dve.wait_ge(s_Hh, T + 1)
                hs = slice(t * P, (t + 1) * P)
                nc.vector.tensor_tensor(H_lo[:, :, hs], tf[:, T % 2], H_hi[:, :, hs].bitcast(F32),
                                        ALU.subtract).then_inc(s_H, 1)

            def gate_sum(T):
                t = T % TPH
                dve.wait_ge(s_gp, T + 1)
                nc.vector.max(top[:, T % 2], M[T % 2][:, 0:NE]).then_inc(s_top, 1)
                dve.wait_ge(s_top, T + 1)
                nc.vector.tensor_tensor(ssum[:, t:t + 1], top[:, T % 2, 0:1], top[:, T % 2, 1:2], ALU.add)\
                    .then_inc(s_sum, 1)
                dve.wait_ge(s_sum, T + 1)
                if T == TPH:
                    dve.wait_ge(s_lats, LC)
                nc.vector.tensor_scalar(sbc[:, t * P:(t + 1) * P], ident[:], ssum[:, t:t + 1], None, ALU.mult)\
                    .then_inc(s_diag, 1)

            def up_square(i):
                dve.wait_ge(s_relu, i + 1)
                nc.vector.tensor_tensor(U[i % 2], U[i % 2], relu[:], ALU.mult).then_inc(s_sq, 1)

            def up_split(i):
                dve.wait_ge(s_Rh, i + 1)
                nc.vector.tensor_tensor(R_lo[:, i % NR], U[i % 2], R_hi[:, i % NR].bitcast(F32),
                                        ALU.subtract).then_inc(s_R, 1)

            def lat_scale(n):
                dve.wait_ge(s_latp, n + 1)
                dve.wait_ge(s_sb, n // LC + 1)
                b = M[(n + 1) % LC]
                nc.vector.tensor_tensor(b, b, sbc[:], ALU.mult).then_inc(s_lats, 1)

            def lat_split(n):
                dve.wait_ge(s_lath, n + 1)
                nc.vector.tensor_tensor(lat_lo[:, n % LC], M[(n + 1) % LC], lat_hi[:, n % LC].bitcast(F32),
                                        ALU.subtract).then_inc(s_lat, 1)

            def group_split(g):
                dve.wait_ge(s_wgh, g + 1)
                for (lo, src), (hi, _) in zip(wg_dst(g, False), wg_dst(g, True)):
                    last = nc.vector.tensor_tensor(lo, src, hi.bitcast(F32), ALU.subtract)
                last.then_inc(s_wg, 1)

            def norm_stats(T):
                dve.wait_ge(s_ffn, T + 1)
                nc.vector.bn_stats(st6[:, T % 2], D[T % TPH]).then_inc(s_bn, 1)
                dve.wait_ge(s_bn, T + 1)
                if T >= TPH:
                    dve.wait_ge(s_ve, T - TPH + 1)
                nc.vector.bn_aggr(mv[:, T % TPH], st6[:, T % 2]).then_inc(s_mv, 1)
                dve.wait_ge(s_mv, T + 1)
                if T == 0:
                    dve.wait_ge(ld_gb, 32)
                nc.vector.scalar_tensor_tensor(D[T % TPH], D[T % TPH], mv[:, T % TPH, 0:1], gamma[:],
                                               ALU.subtract, ALU.mult).then_inc(s_cen, 1)

            def norm_apply(T):
                dve.wait_ge(s_rstd, T + 1)
                dve.wait_ge(s_cen, T + 1)
                dve.wait_ge(s_xb, T + 1)
                nc.vector.scalar_tensor_tensor(X[:, T, :], D[T % TPH], rstd[:, T % TPH:T % TPH + 1], X[:, T, :],
                                               ALU.mult, ALU.add).then_inc(s_x1, 1)

            nc.vector.memset(ones[:], 1.0).then_inc(s_ones, 1)
            dve.wait_ge(s_cTp, 1)
            nc.vector.tensor_copy(cT[:], M[0][:, 0:N]).then_inc(s_cT, 1)
            dve.wait_ge(s_cT, 1)
            nc.vector.tensor_tensor(prod0[:], bcast_mid(M[0][:, N:N + C], N),
                                    cT[:].unsqueeze(2).broadcast_to([CD, N, C]), ALU.mult).then_inc(s_prod0, 1)
            dve.wait_ge(s_prod0, 1)
            dve.wait_ge(ld_c, 48)
            nc.vector.tensor_tensor(prod0[0:1], prod0[0:1], bcast_mid(fside[:], N), ALU.add).then_inc(s_prod0, 1)
            dve.wait_ge(ld_wc, 16 * G)
            dve.wait_ge(s_zero, 1)
            for j in range(PH):
                e = 2 * PADK + j
                nc.vector.tensor_copy(wc_pad[C * j:C * (j + 1), :, j:e + 1], wc_nat[:, :, ::-1]).then_inc(s_wcp, 1)
            dve.wait_ge(s_blk, 3)
            nc.vector.reduce_sum(gmask[:], blk[:].rearrange("p j g -> p g j"), AX_X).then_inc(s_gmask, 1)
            dve.wait_ge(s_wcp, PH)
            dve.wait_ge(s_gmask, 1)
            for a in range(NWIN):
                e = 2 * PADK - PH * a
                nc.vector.tensor_tensor(
                    wconv[:, a].rearrange("p (f g o) -> p f g o", f=PH, g=G),
                    wc_pad[:, :, e:e + PH].rearrange("p o f -> p f o").unsqueeze(2).broadcast_to([P, PH, G, CG]),
                    gmask[:].unsqueeze(1).unsqueeze(3).broadcast_to([P, PH, G, CG]), ALU.mult).then_inc(s_wconv, 1)
            dve.wait_ge(ld_x[0], 16)
            shift_copies(0, 2)
            dve.wait_ge(ld_x[1], 16)
            shift_copies(2, 4)
            add_ctx(0)
            split_up(0)
            split_H(0)
            add_ctx(1)
            split_up(1)
            split_H(1)
            dve.wait_ge(s_lgp, 1)
            nc.vector.tensor_tensor(att[:, 0, :], D[0][0:N, 0:KE], b2[:], ALU.add).then_inc(s_att, 1)
            dve.wait_ge(s_att, 1)
            nc.vector.reduce_max(att[:, 3, 1:2], att[:, 0, :], AX_X).then_inc(s_att, 1)
            dve.wait_ge(s_att, 2)
            nc.vector.tensor_scalar(att[:, 1, :], att[:, 0, :], att[:, 3, 1:2], None, ALU.subtract).then_inc(s_att, 1)
            gate_sum(0)
            add_ctx(2)
            dve.wait_ge(s_aexp, 1)
            nc.vector.reciprocal(att[:, 3, 2:3], att[:, 3, 0:1]).then_inc(s_att, 1)
            dve.wait_ge(s_att, 4)
            nc.vector.tensor_scalar(att[:, 0, :], att[:, 2, :], att[:, 3, 2:3], None, ALU.mult).then_inc(s_att, 1)
            split_H(2)
            split_up(2)
            gate_sum(1)
            for i in range(LC):
                dve.wait_ge(s_E2h, i + 1)
                nc.vector.tensor_tensor(ex_lo[:, i, :], (D[3], M[1])[i], ex_hi[:, i, :].bitcast(F32),
                                        ALU.subtract).then_inc(s_E2, 1)
            add_ctx(3)
            split_H(3)
            dve.wait_ge(s_aT, 1)
            nc.vector.tensor_tensor(prod1[:], bcast_mid(bk[:], N), attT[:].unsqueeze(2).broadcast_to([KE, N, C]),
                                    ALU.mult).then_inc(s_prod1, 1)
            split_up(3)
            gate_sum(2)
            gate_sum(3)
            for h in range(HALVES):
                T0, i0 = h * TPH, h * IC
                if h:
                    for t in range(TPH):
                        if t < 2:
                            norm_stats(t)
                        add_ctx(T0 + t)
                        if t < 2:
                            norm_apply(t)
                        if t:
                            gate_sum(T0 + t - 1)
                        split_H(T0 + t)
                    gate_sum(T0 + TPH - 1)
                up_square(i0)
                up_split(i0)
                if h:
                    norm_stats(2)
                    norm_apply(2)
                else:
                    split_up(4)
                up_square(i0 + 1)
                up_split(i0 + 1)
                if h:
                    norm_stats(3)
                    norm_apply(3)
                else:
                    split_up(5)
                for n in range(LC):
                    lat_scale(h * LC + n)
                    lat_split(h * LC + n)
                    if not h:
                        split_up(6 + n)
                for c in range(2, IC):
                    up_square(i0 + c)
                    up_split(i0 + c)
                    if h == 0:
                        if c == 3:
                            dve.wait_ge(ld_x[2], 16)
                            dve.wait_ge(ld_x[3], 16)
                            shift_copies(TPH, TILES)
                    else:
                        group_split(c - 2)
                if h:
                    for g in range(IC - 2, len(wgroups)):
                        group_split(g)

            def y_bias(T):
                dve.wait_ge(s_yp, T + 1)
                b = M[T % 2].rearrange("p (c t) -> p c t", c=PH)
                nc.vector.tensor_tensor(b, b, bcast_mid(B1[:, T * P:(T + 1) * P], PH), ALU.add).then_inc(s_yb, 1)

            def y_split(T):
                hs = slice(T % TPH * P, (T % TPH + 1) * P)
                dve.wait_ge(s_Yh, T + 1)
                nc.vector.tensor_tensor(H_lo[:, :, hs], M[T % 2].rearrange("p (c t) -> p c t", c=PH),
                                        H_hi[:, :, hs].bitcast(F32), ALU.subtract).then_inc(s_Y, 1)

            def scores(T):
                s = sm[:, T % 2]
                dve.wait_ge(s_q, T + 1)
                nc.vector.tensor_tensor(pr[:], QK[T % 2][1][:, 0:QW], qs[:], ALU.mult).then_inc(s_pr, 1)
                dve.wait_ge(s_pr, T + 1)
                nc.vector.reduce_sum(s[:, 0, :], pr[:].rearrange("p (e d) -> p e d", e=E), AX_X).then_inc(s_sc, 1)
                dve.wait_ge(s_sc, T + 1)
                nc.vector.reduce_max(s[:, 1, 0:1], s[:, 0, :], AX_X).then_inc(s_mx, 1)
                dve.wait_ge(s_mx, T + 1)
                nc.vector.tensor_scalar(s[:, 1, 1:2], s[:, 1, 0:1], -SCALE, None, ALU.mult).then_inc(s_nmx, 1)

            def weigh(T):
                s = sm[:, T % 2]
                dve.wait_ge(s_e, T + 1)
                nc.vector.reciprocal(s[:, 3, 1:2], s[:, 3, 0:1]).then_inc(s_rc, 1)
                dve.wait_ge(s_rc, T + 1)
                if T:
                    dve.wait_ge(s_hwp, T)
                for a in range(2):
                    last = nc.vector.scalar_tensor_tensor(
                        hw[:, a * HH:(a + 1) * HH].rearrange("p (e r) -> p e r", e=EH),
                        QK[T % 2][a][:, QW:QKW].rearrange("p (e r) -> p e r", e=EH), s[:, 3, 1:2],
                        s[:, 2, a * EH:(a + 1) * EH].unsqueeze(2).broadcast_to([P, EH, R]), ALU.mult, ALU.mult)
                last.then_inc(s_hw, 1)

            def hw_split(T):
                dve.wait_ge(s_hwh, T + 1)
                nc.vector.tensor_tensor(hwT_lo[:, T % 2], QK[T % 2][0][:, 0:P], hwT_hi[:, T % 2].bitcast(F32),
                                        ALU.subtract).then_inc(s_hwT, 1)

            def finish(T):
                dve.wait_ge(s_res, T + 1)
                dve.wait_ge(s_x1b, T + 1)
                nc.vector.tensor_tensor(X[:, T, :], D[T % TPH], X[:, T, :], ALU.add).then_inc(s_fin, 1)

            for h in range(HALVES):
                for t in range(TPH):
                    T = h * TPH + t
                    y_bias(T)
                    if h == 0:
                        norm_stats(TPH + t)
                    elif t == 0:
                        finish(T - 1)
                    y_split(T)
                    if h == 0:
                        norm_apply(TPH + t)
                for t in range(TPH):
                    T = h * TPH + t
                    scores(T)
                    if t:
                        finish(T - 1)
                    weigh(T)
                    hw_split(T)
            finish(TILES - 1)

        @block.tensor
        def _(pe):
            def mm3(o, lh, ll, rh, rl, start, stop):
                nc.tensor.matmul(o, lh, rh, start=start, stop=False)
                nc.tensor.matmul(o, lh, rl, start=False, stop=False)
                return nc.tensor.matmul(o, ll, rh, start=False, stop=stop)

            def conv(T):
                if T >= 2:
                    pe.wait_ge(s_tf, T - 1)
                if T >= TPH:
                    pe.wait_ge(s_R, IC)
                for s in range(SPT):
                    for a in range(NWIN):
                        last = nc.tensor.matmul(U[T % 2][:, s * P:(s + 1) * P],
                                                XS[:, T % TPH * SPT + s, a:a + P], wconv[:, a],
                                                start=(a == 0), stop=(a == NWIN - 1))
                last.then_inc(s_conv, 1)

            def gate_logits(T):
                pe.wait_ge(s_tf, T + 1)
                if T == 0:
                    pe.wait_ge(ld_gate, 16)
                if T >= 2:
                    pe.wait_ge(s_top, T - 1)
                if T == TPH:
                    pe.wait_ge(s_lat, LC)
                if T == 3:
                    pe.wait_ge(s_E2, 2)
                for p in range(PH):
                    last = nc.tensor.matmul(M[T % 2][:, 0:NE], tf[:, T % 2, p], gate[:, p],
                                            start=(p == 0), stop=(p == PH - 1))
                last.then_inc(s_gp, 1)

            def up(i):
                h, c = divmod(i, IC)
                if h == 0:
                    pe.wait_ge(s_up, c + 1)
                if c == 0:
                    pe.wait_ge(s_H, TPH * (h + 1))
                if i >= 2:
                    pe.wait_ge(s_R, i - 1)
                for p in range(PH):
                    last = mm3(U[i % 2], up_hi[:, c, p], up_lo[:, c, p], H_hi[:, p], H_lo[:, p],
                               p == 0, p == PH - 1)
                last.then_inc(s_upp, 1)

            def scale_rows(h):
                pe.wait_ge(s_diag, TPH * (h + 1))
                for t in range(TPH):
                    last = nc.tensor.matmul(M[0][:, t * P:(t + 1) * P], ones[:], sbc[:, t * P:(t + 1) * P],
                                            start=True, stop=True)
                last.then_inc(s_sbp, 1)

            def latent(n):
                h, c = divmod(n, LC)
                if c == 0:
                    pe.wait_ge(s_top, TPH * (h + 1))
                else:
                    pe.wait_ge(s_sb, h + 1)
                if h == 0:
                    pe.wait_ge(s_fc, 1)
                for p in range(PH):
                    last = mm3(M[(n + 1) % LC], fc_hi[:, p, c * P:(c + 1) * P], fc_lo[:, p, c * P:(c + 1) * P],
                               H_hi[:, p], H_lo[:, p], p == 0, p == PH - 1)
                last.then_inc(s_latp, 1)

            def down(i):
                h, c = divmod(i, IC)
                pe.wait_ge(s_R, i + 1)
                if h == 0:
                    pe.wait_ge(s_dn, c + 1)
                for t in range(TPH):
                    if h and c == 0:
                        pe.wait_ge(s_x1, t + 1)
                    if h == 0 and c == 0:
                        pe.wait_ge(s_BD, 1)
                        pe.wait_ge(s_B1, 2)
                        pe.wait_ge(s_E2, 2)
                    ts = slice(t * P, (t + 1) * P)
                    last = mm3(D[t], R_hi[:, i % NR, ts], R_lo[:, i % NR, ts], dn_hi[:, c], dn_lo[:, c],
                               c == 0, c == IC - 1)
                    if c == IC - 1:
                        last.then_inc(s_ffn, 1)
                    elif t == TPH - 1:
                        last.then_inc(s_down, 1)

            def routed(h):
                pe.wait_ge(s_lat, LC * (h + 1))
                for t in range(TPH):
                    ts = slice(t * P, (t + 1) * P)
                    for c in range(LC):
                        mm3(D[t], lat_hi[:, c, ts], lat_lo[:, c, ts], ex_hi[:, c], ex_lo[:, c], False, False)

            def turn_group(g):
                what, p = wgroups[g]
                if g >= 2:
                    pe.wait_ge(s_wg, g - 1)
                if g == 0:
                    pe.wait_ge(ld_w, 16)
                if what == "a":
                    pe.wait_ge(ld_ab, 16 * (1 + PH))
                if what == "qk" and p == 0:
                    pe.wait_ge(ld_qk, 32)
                ps = slice(p * P, (p + 1) * P)
                src = {
                    "w": lambda k: w_raw[:, k, ps],
                    "qk": lambda k: qk_raw[:, k // LC, k % LC, ps],
                    "a": lambda k: a_raw[:, k * P:(k + 1) * P],
                    "b": lambda k: b_raw[:, k].rearrange("p e r -> p (e r)"),
                }[what]
                for k in range(PH):
                    last = nc.tensor.transpose(M[g % 2][:, k * P:(k + 1) * P], src(k), ident[:])
                last.then_inc(s_wgp, 1)

            pe.wait_ge(s_ident, 2)
            pe.wait_ge(ld_c, 48)
            nc.tensor.transpose(M[0][:, 0:N], c_nat[:], ident[0:N, 0:N])
            nc.tensor.transpose(M[0][:, N:N + C], cw_nat[:], ident[0:C, 0:C]).then_inc(s_cTp, 1)
            pe.wait_ge(s_cT, 1)
            pe.wait_ge(s_ones, 1)
            pe.wait_ge(s_prod0, 2)
            pf = prod0[:].rearrange("d n o -> d (n o)")
            for i in range(2):
                nc.tensor.matmul(D[i], ones[:], pf[:, i * BANK:(i + 1) * BANK], start=True, stop=True)\
                    .then_inc(s_B0p, 1)
            pe.wait_ge(ld_cond, 16 * 8)
            pe.wait_ge(s_B0, 1)
            nc.tensor.matmul(D[0][:, 0:N], W0[:], cT[:], start=True, stop=True).then_inc(s_c1p, 1)
            pe.wait_ge(s_wconv, NWIN)
            pe.wait_ge(s_zero, 2)
            pe.wait_ge(xs_v, 1)
            pe.wait_ge(xs_a, 1)
            conv(0)
            pe.wait_ge(s_c1, 1)
            pe.wait_ge(s_B0, 2)
            nc.tensor.matmul(D[1][:, 0:N], W1[:], h1[:], start=True, stop=True).then_inc(s_c2p, 1)
            conv(1)
            gate_logits(0)
            pe.wait_ge(ld_ex, 16)
            for mc in range(LC):
                for lc in range(LC):
                    last = nc.tensor.transpose(D[2][:, mc * LAT + lc * P:mc * LAT + (lc + 1) * P],
                                               exraw[:, lc, mc * P:(mc + 1) * P], ident[:])
            last.then_inc(s_exTp, 1)
            pe.wait_ge(s_c2, 1)
            nc.tensor.matmul(D[0][0:N, 0:KE], h2[:], W2[:], start=True, stop=True).then_inc(s_lgp, 1)
            pe.wait_ge(xs_v, 2)
            pe.wait_ge(xs_a, 2)
            conv(2)
            gate_logits(1)
            pe.wait_ge(s_exT, 1)
            pe.wait_ge(ld_fc2, 16)
            for lc in range(LC):
                if lc:
                    pe.wait_ge(s_top, 2)
                for mc in range(LC):
                    last = nc.tensor.matmul((D[3], M[1])[lc], exT[:, mc, lc * P:(lc + 1) * P], fc2[:, mc],
                                            start=(mc == 0), stop=(mc == LC - 1))
                last.then_inc(s_E2p, 1)
            conv(3)
            pe.wait_ge(s_att, 5)
            nc.tensor.transpose(D[0][0:KE, 0:N], att[:, 0, :], ident[0:N, 0:N]).then_inc(s_aTp, 1)
            gate_logits(2)
            gate_logits(3)
            pe.wait_ge(s_aT, 1)
            for o in range(C):
                last = nc.tensor.matmul(D[o // (C // 2)][0:C, o % (C // 2) * N:(o % (C // 2) + 1) * N],
                                        wk[:, o], attT[:], start=True, stop=True)
            last.then_inc(s_AGp, 1)
            pe.wait_ge(s_prod1, 1)
            pe.wait_ge(s_exT, 1)
            pf1 = prod1[:].rearrange("k n o -> k (n o)")
            for i in range(2):
                if i:
                    pe.wait_ge(s_E2, 1)
                nc.tensor.matmul(D[2 + i], ones[0:KE, :], pf1[:, i * BANK:(i + 1) * BANK], start=True, stop=True)\
                    .then_inc(s_B1p, 1)
            for h in range(HALVES):
                if h:
                    pe.wait_ge(xs_v, 3)
                    pe.wait_ge(xs_a, 3)
                    for t in range(TPH):
                        conv(TPH + t)
                        if t:
                            gate_logits(TPH + t - 1)
                    gate_logits(TILES - 1)
                up(h * IC)
                up(h * IC + 1)
                scale_rows(h)
                for n in range(LC):
                    latent(h * LC + n)
                for c in range(IC):
                    if c + 2 < IC:
                        up(h * IC + c + 2)
                    down(h * IC + c)
                    if c == 0:
                        routed(h)
                    if h and c >= 1 and c < IC - 1:
                        turn_group(c - 1)
                if h:
                    for g in range(IC - 2, len(wgroups)):
                        turn_group(g)

            def mix(T):
                pe.wait_ge(s_x1, T + 1)
                if T >= 2:
                    pe.wait_ge(s_Y, T - 1)
                if T == 0:
                    pe.wait_ge(s_BD, 1)
                    pe.wait_ge(s_wg, len(wgroups))
                if T == TPH:
                    pe.wait_ge(s_hwT, TPH)
                for p in range(PH):
                    last = nc.tensor.matmul(M[T % 2][:, p * P:(p + 1) * P], X[:, T, p * P:(p + 1) * P], BD[:, T],
                                            start=True, stop=True)
                last.then_inc(s_yp, 1)

            def qk(T):
                ts = slice(T % TPH * P, (T % TPH + 1) * P)
                pe.wait_ge(s_Y, T + 1)
                if T % TPH in (1, ):
                    pe.wait_ge(s_Y, T - T % TPH + TPH)
                if T >= 2:
                    pe.wait_ge(s_hwT, T - 1)
                for a in range(2):
                    for p in range(PH):
                        last = mm3(QK[T % 2][a][:, 0:QKW], H_hi[:, p, ts], H_lo[:, p, ts],
                                   qkT_hi[:, p, a], qkT_lo[:, p, a], p == 0, p == PH - 1)
                last.then_inc(s_qkp, 1)

            def dense(T):
                ts = slice(T % TPH * P, (T % TPH + 1) * P)
                if T < TPH:
                    pe.wait_ge(s_x1, TPH + T + 1)
                else:
                    pe.wait_ge(s_fin, T - TPH + 1)
                for p in range(PH):
                    mm3(D[T % TPH], H_hi[:, p, ts], H_lo[:, p, ts], wT_hi[:, p], wT_lo[:, p], p == 0, False)

            def turn_hw(T):
                pe.wait_ge(s_hw, T + 1)
                nc.tensor.transpose(QK[T % 2][0][:, 0:P], hw[:], ident[:]).then_inc(s_hwp, 1)

            def combine(T):
                pe.wait_ge(s_hwT, T + 1)
                mm3(D[T % TPH], hwT_hi[:, T % 2], hwT_lo[:, T % 2], bT_hi[:], bT_lo[:], False, True)\
                    .then_inc(s_res, 1)

            for h in range(HALVES):
                for t in range(TPH):
                    mix(h * TPH + t)
                for t in range(TPH):
                    T = h * TPH + t
                    qk(T)
                    if t:
                        combine(T - 1)
                    dense(T)
                    turn_hw(T)
                combine(h * TPH + TPH - 1)


_INS = ['x', 'cond_128', 'fside_S_0', 'L0_cond_weight', 'L0_cond_c_weight', 'L0_ffn_gate_w', 'L0_ffn_up_w',
        'L0_ffn_down_w', 'L0_ffn_fc1_w', 'L0_ffn_fc2_w', 'L0_ffn_expert_w', 'L0_ffn_ln_gamma', 'L0_ffn_ln_beta',
        'L1_cond_W0', 'L1_cond_b0', 'L1_cond_W1', 'L1_cond_b1', 'L1_cond_W2', 'L1_cond_b2', 'L1_cond_weight',
        'L1_cond_bias_k', 'L1_ffn_W', 'L1_ffn_b', 'L1_ffn_Wq', 'L1_ffn_Wk', 'L1_ffn_A', 'L1_ffn_Bm']
_OUTS = [((32, 32, 512), 'float32')]


def kernel(**inputs):
    import numpy as _np
    import concourse.bacc as _bacc
    from concourse import mybir as _mybir
    from concourse.bass_utils import run_bass_kernel_spmd as _run

    nc = _bacc.Bacc("TRN2", target_bir_lowering=False, num_devices=1, dynamic_dma_scratch_size=4096)
    arrays, args = {}, []
    for name in _INS:
        a = _np.ascontiguousarray(inputs[name])
        arrays[f"in_{name}_dram"] = a
        args.append(nc.dram_tensor(f"in_{name}_dram", a.shape, _mybir.dt.from_np(a.dtype), kind="ExternalInput").ap())
    for i, (shape, dtype) in enumerate(_OUTS):
        dt = _mybir.dt.from_np(_np.dtype(dtype))
        args.append(nc.dram_tensor(f"out_{i}_dram", shape, dt, kind="ExternalOutput").ap())
    bass_adaln_ffn(nc, *args)
    r = _run(nc, [arrays], core_ids=[0])
    got = tuple(r.results[0][f"out_{i}_dram"] for i in range(len(_OUTS)))
    return got[0]
```

```python
import math
from contextlib import ExitStack

import concourse.bass as bass
from concourse import mybir

F32 = mybir.dt.float32
F32R = mybir.dt.float32r
ALU = mybir.AluOpType
ACT = mybir.ActivationFunctionType
AX_X = mybir.AxisListType.X

P = 128
BANK = 512


def bass_adaln_ffn(
    nc: bass.Bass,
    x: bass.AP,
    cond_128: bass.AP,
    fside_S_0: bass.AP,
    L0_cond_weight: bass.AP,
    L0_cond_c_weight: bass.AP,
    L0_ffn_gate_w: bass.AP,
    L0_ffn_up_w: bass.AP,
    L0_ffn_down_w: bass.AP,
    L0_ffn_fc1_w: bass.AP,
    L0_ffn_fc2_w: bass.AP,
    L0_ffn_expert_w: bass.AP,
    L0_ffn_ln_gamma: bass.AP,
    L0_ffn_ln_beta: bass.AP,
    L1_cond_W0: bass.AP,
    L1_cond_b0: bass.AP,
    L1_cond_W1: bass.AP,
    L1_cond_b1: bass.AP,
    L1_cond_W2: bass.AP,
    L1_cond_b2: bass.AP,
    L1_cond_weight: bass.AP,
    L1_cond_bias_k: bass.AP,
    L1_ffn_W: bass.AP,
    L1_ffn_b: bass.AP,
    L1_ffn_Wq: bass.AP,
    L1_ffn_Wk: bass.AP,
    L1_ffn_A: bass.AP,
    L1_ffn_Bm: bass.AP,
    out: bass.AP,
):
    N, C, L = x.shape
    CD = cond_128.shape[1]
    INT = L0_ffn_up_w.shape[1]
    LAT = L0_ffn_fc1_w.shape[1]
    NE = L0_ffn_gate_w.shape[1]
    KT = L0_cond_weight.shape[2]
    CG = L0_cond_weight.shape[1]
    KE, CHID = L1_cond_W2.shape[1], L1_cond_W0.shape[1]
    E, R, _ = L1_ffn_A.shape
    DK = L1_ffn_Wq.shape[0] // E
    EPS = 1e-5

    SPT = P // C
    TILES = N // SPT
    HALVES = 2
    TPH = TILES // HALVES
    NPH = N // HALVES
    TOKH = TPH * P
    PH = L // P
    IC = INT // P
    LC = LAT // P
    G = C // CG
    QW = E * DK
    HH = E * R // 2
    EH = E // 2
    QKW = QW + HH
    NWIN = 3
    PADK = KT // 2
    XW = P + 2
    SCALE = 1.0 / math.sqrt(DK)
    assert L == BANK and TOKH == BANK and PH == 4 and C == 32 and KT == 9 and 2 * QKW == 640
    NR = 3

    xt_dram = x.rearrange("(t s) c l -> (s c) t l", s=SPT)
    out_dram = out.rearrange("(t s) c l -> (s c) t l", s=SPT)

    with ExitStack() as ctx:
        def sb(name, shape, dt=F32, scope=ctx):
            return scope.enter_context(nc.sbuf_tensor(name, shape, dt))

        def sem(name):
            return ctx.enter_context(nc.semaphore(name))

        PS = ctx.enter_context(nc.psum_tensor("PS", [P, 8, BANK], F32))
        D = [PS[:, b, :] for b in range(4)]
        U = [PS[:, 4, :], PS[:, 5, :]]
        M = [PS[:, 6, :], PS[:, 7, :]]
        QK = [(U[0], U[1]), (M[0], M[1])]

        ident = sb("ident", [P, P])
        ones = sb("ones", [P, P])
        X = sb("X", [P, TILES, L])
        XS = sb("XS", [P, NPH, XW])
        wconv = sb("wconv", [P, NWIN, P])
        up_hi = sb("up_hi", [P, IC, PH, P], F32R)
        up_lo = sb("up_lo", [P, IC, PH, P], F32R)
        dn_hi = sb("dn_hi", [P, IC, L], F32R)
        dn_lo = sb("dn_lo", [P, IC, L], F32R)
        fc_hi = sb("fc_hi", [P, PH, LAT], F32R)
        fc_lo = sb("fc_lo", [P, PH, LAT], F32R)
        ex_hi = sb("ex_hi", [P, LC, L], F32R)
        ex_lo = sb("ex_lo", [P, LC, L], F32R)
        gate = sb("gate", [P, PH, NE])
        gate_hl = sb("gate_hl", [P, PH, P], F32R)
        fold = sb("fold", [2 * NE, NE])
        gamma = sb("gamma", [P, L])
        rowb = sb("rowb", [P, L])
        B0 = sb("B0", [P, N * C])
        B1 = sb("B1", [P, N * C])
        BD = sb("BD", [P, TILES, P])
        H_hi = sb("H_hi", [P, PH, TOKH], F32R)
        H_lo = sb("H_lo", [P, PH, TOKH], F32R)
        tf = sb("tf", [P, 2, PH, P])
        sbc = sb("sbc", [P, TOKH])
        top = sb("top", [P, TPH, 8])
        ssum = sb("ssum", [P, TPH])
        st6 = sb("st6", [P, 2, 6])
        mv = sb("mv", [P, TPH, 2])
        ve = sb("ve", [P, TPH])
        nhalf = sb("nhalf", [P, 1])
        rstd = sb("rstd", [P, TPH])
        qk_raw = sb("qk_raw", [P, 2, LC, L])
        qs = sb("qs", [P, QW])
        pr = sb("pr", [P, QW])
        hw = sb("hw", [P, P])
        hwT_hi = sb("hwT_hi", [P, 2, P], F32R)
        hwT_lo = sb("hwT_lo", [P, 2, P], F32R)
        sm = sb("sm", [P, 2, 4, E])

        with ExitStack() as early:
            def se(name, shape):
                return sb(name, shape, F32, early)
            c_nat = se("c_nat", [N, CD])
            cw_nat = se("cw_nat", [C, CD])
            cT = se("cT", [CD, N])
            prod0 = se("prod0", [CD, N, C])
            fsb = se("fsb", [P, C])
            wc_nat = se("wc_nat", [C, CG, KT])
            wc_pad = se("wc_pad", [C, NWIN * PH + PH - 1, C])
            gmask = se("gmask", [C, G])
            exraw = se("exraw", [P, LC, LAT])
            exT = se("exT", [P, LC, LAT])
            W0 = se("W0", [CD, CHID])
            W1 = se("W1", [CHID, CHID])
            W2 = se("W2", [CHID, KE])
            b0 = se("b0", [CHID, 1])
            b1 = se("b1", [CHID, 1])
            b2 = se("b2", [N, KE])
            h1 = se("h1", [CHID, N])
            h2 = se("h2", [CHID, N])
            att = se("att", [N, 4, KE])
            attT = se("attT", [KE, N])
            wk = se("wk", [KE, C, C])
            bk = se("bk", [KE, C])
            prod1 = se("prod1", [KE, N, C])
            agg = prod0[0:C]
        relu = sb("relu", [P, TOKH])
        R_hi = sb("R_hi", [P, NR, TOKH], F32R)
        R_lo = sb("R_lo", [P, NR, TOKH], F32R)
        lat_hi = sb("lat_hi", [P, LC, TOKH], F32R)
        lat_lo = sb("lat_lo", [P, LC, TOKH], F32R)

        with ExitStack() as raw:
            up_raw = sb("up_raw", [P, PH, INT], F32, raw)
            dn_raw = sb("dn_raw", [P, IC, L], F32, raw)
            fc_raw = sb("fc_raw", [P, PH, LAT], F32, raw)
            fc2 = sb("fc2", [P, LC, L], F32, raw)
        wT_hi = sb("wT_hi", [P, PH, L], F32R)
        wT_lo = sb("wT_lo", [P, PH, L], F32R)
        qkT_hi = sb("qkT_hi", [P, PH, 2, QKW], F32R)
        qkT_lo = sb("qkT_lo", [P, PH, 2, QKW], F32R)
        bT_hi = sb("bT_hi", [P, L], F32R)
        bT_lo = sb("bT_lo", [P, L], F32R)

        w_raw = XS[:].rearrange("p n w -> p (n w)")[:, 0:PH * L].rearrange("p (c l) -> p c l", c=PH)
        tflat = tf[:].rearrange("p a b c -> p (a b c)")
        a_raw = tflat[:, 0:L]
        b_raw = tflat[:, L:2 * L].rearrange("p (c e r) -> p c e r", c=PH, e=E)

        ld_c = sem("ld_c")
        ld_fs = sem("ld_fs")
        ld_wc = sem("ld_wc")
        ld_x = [sem(f"ld_x{i}") for i in range(4)]
        ld_ex = sem("ld_ex")
        ld_fc2 = sem("ld_fc2")
        ld_up = [sem(f"ld_up{i}") for i in range(2)]
        ld_fc = sem("ld_fc")
        ld_gate = sem("ld_gate")
        ld_dn = [sem(f"ld_dn{i}") for i in range(2)]
        ld_cond = sem("ld_cond")
        ld_gb = sem("ld_gb")
        ld_b = sem("ld_b")
        ld_w = sem("ld_w")
        ld_qk = sem("ld_qk")
        ld_ab = sem("ld_ab")
        s_ones = sem("s_ones")
        s_ident = sem("s_ident")
        s_zero = sem("s_zero")
        s_gmask = sem("s_gmask")
        s_cTp = sem("s_cTp")
        s_cT = sem("s_cT")
        s_prod0 = sem("s_prod0")
        s_wcp = sem("s_wcp")
        s_wcT = sem("s_wcT")
        s_wconv = sem("s_wconv")
        s_B0p = sem("s_B0p")
        s_B0 = sem("s_B0")
        s_exTp = sem("s_exTp")
        s_exT = sem("s_exT")
        s_E2p = sem("s_E2p")
        s_E2h = sem("s_E2h")
        s_E2 = sem("s_E2")
        s_c1p = sem("s_c1p")
        s_c1 = sem("s_c1")
        s_c2p = sem("s_c2p")
        s_c2 = sem("s_c2")
        s_lgp = sem("s_lgp")
        s_att = sem("s_att")
        s_aexp = sem("s_aexp")
        s_aTp = sem("s_aTp")
        s_aT = sem("s_aT")
        s_prod1 = sem("s_prod1")
        s_AGp = sem("s_AGp")
        s_agg = sem("s_agg")
        s_BD = sem("s_BD")
        s_B1p = sem("s_B1p")
        s_B1 = sem("s_B1")
        s_uph = sem("s_uph")
        s_up = sem("s_up")
        s_fch = sem("s_fch")
        s_fc = sem("s_fc")
        s_dnh = sem("s_dnh")
        s_dn = sem("s_dn")
        s_wgp = sem("s_wgp")
        s_wgh = sem("s_wgh")
        s_wg = sem("s_wg")
        xs_v = sem("xs_v")
        xs_a = sem("xs_a")
        s_conv = sem("s_conv")
        s_tf = sem("s_tf")
        s_Hh = sem("s_Hh")
        s_H = sem("s_H")
        s_gatez = sem("s_gatez")
        s_gateh = sem("s_gateh")
        s_gate = sem("s_gate")
        s_fold = sem("s_fold")
        s_gT = sem("s_gT")
        s_gTs = sem("s_gTs")
        s_gp = sem("s_gp")
        s_top = sem("s_top")
        s_sum = sem("s_sum")
        s_diag = sem("s_diag")
        s_sbp = sem("s_sbp")
        s_sb = sem("s_sb")
        s_latp = sem("s_latp")
        s_lats = sem("s_lats")
        s_lath = sem("s_lath")
        s_lat = sem("s_lat")
        s_upp = sem("s_upp")
        s_relu = sem("s_relu")
        s_sq = sem("s_sq")
        s_Rh = sem("s_Rh")
        s_R = sem("s_R")
        s_down = sem("s_down")
        s_ffn = sem("s_ffn")
        s_bn = sem("s_bn")
        s_mv = sem("s_mv")
        s_ve = sem("s_ve")
        s_rstd = sem("s_rstd")
        s_cen = sem("s_cen")
        s_x1 = sem("s_x1")
        s_xb = sem("s_xb")
        s_yp = sem("s_yp")
        s_yb = sem("s_yb")
        s_Yh = sem("s_Yh")
        s_Y = sem("s_Y")
        s_x1b = sem("s_x1b")
        s_qkp = sem("s_qkp")
        s_q = sem("s_q")
        s_pr = sem("s_pr")
        s_sc = sem("s_sc")
        s_mx = sem("s_mx")
        s_nmx = sem("s_nmx")
        s_e = sem("s_e")
        s_rc = sem("s_rc")
        s_hw = sem("s_hw")
        s_hwp = sem("s_hwp")
        s_hwh = sem("s_hwh")
        s_hwT = sem("s_hwT")
        s_res = sem("s_res")
        s_fin = sem("s_fin")
        s_out = sem("s_out")

        block = ctx.enter_context(nc.Block())

        wgroups = [("qk", p) for p in range(PH)] + [("w", p) for p in range(PH)] + [("a", 0), ("b", 0)]
        GCONV = len(wgroups) - IC + 2

        def wg_dst(g, hi):
            what, p = wgroups[g]
            if what == "w":
                return [((wT_hi if hi else wT_lo)[:, p, :], M[g % 2])]
            if what == "b":
                return [((bT_hi if hi else bT_lo)[:], M[g % 2])]
            t = qkT_hi if hi else qkT_lo
            if what == "qk":
                return [(t[:, p, :, 0:QW], M[g % 2].rearrange("p (a q) -> p a q", a=2))]
            return [(t[:, :, a, QW:QKW],
                     M[g % 2].rearrange("p (c a q) -> p a c q", c=PH, a=2)[:, a]) for a in range(2)]

        def conv_groups(t):
            return {1: [0], 2: [1], 3: range(2, GCONV)}.get(t, [])

        def mix_bank(T):
            return (M[T] if T < 2 else D[T % TPH]).rearrange("p (c t) -> p c t", c=PH)

        def bcast_mid(ap, n):
            return ap.unsqueeze(1).broadcast_to([ap.shape[0], n, *ap.shape[1:]])

        def down_done(eng, i):
            h, c = divmod(i, IC)
            if c == IC - 1:
                eng.wait_ge(s_ffn, TPH * (h + 1))
            else:
                eng.wait_ge(s_down, h * (IC - 1) + c + 1)

        XPARTS = [(0, 1), (1, 2), (2, TPH), (TPH, TILES)]

        def phase_copies(eng, t0, t1):
            for s in range(SPT):
                for j in range(PH):
                    if (PH * s + j < 10) == (eng is nc.vector):
                        last = phase_copy(eng, s, j, t0, t1)
            return last

        def phase_copy(eng, s, j, t0, t1):
            src = X[C * s:C * (s + 1), t0:t1, :].rearrange("p t (m j) -> p t m j", j=PH)[:, :, :, j]
            a, b = t0 % TPH, (t1 - 1) % TPH + 1
            dst = XS[C * j:C * (j + 1), a * SPT:b * SPT, 1:1 + P]\
                .rearrange("p (t s) m -> p t s m", s=SPT)[:, :, s]
            if eng is nc.vector:
                return nc.vector.tensor_copy(dst, src)
            return nc.scalar.activation(dst, src, ACT.Copy)

        @block.sync
        def _(sp):
            def load_x(i):
                t0, t1 = XPARTS[i]
                sp.dma_start(X[:, t0:t1, :], xt_dram[:, t0:t1, :]).then_inc(ld_x[i], 16)

            sp.dma_start(c_nat[:], cond_128).then_inc(ld_c, 16)
            for i in range(3):
                load_x(i)
            for dst, src in ((W0, L1_cond_W0), (W1, L1_cond_W1), (W2, L1_cond_W2), (bk, L1_cond_bias_k)):
                sp.dma_start(dst[:], src).then_inc(ld_cond, 16)
            for dst, src in ((b0, L1_cond_b0), (b1, L1_cond_b1)):
                sp.dma_start(dst[:], src.rearrange("(p a) -> p a", a=1)).then_inc(ld_cond, 16)
            sp.dma_start(b2[:], L1_cond_b2.partition_broadcast(N)).then_inc(ld_cond, 16)
            sp.dma_start(wk[:], L1_cond_weight.rearrange("k o i a -> k o (i a)")).then_inc(ld_cond, 16)
            sp.dma_start(exraw[:], L0_ffn_expert_w.rearrange("(c p) m -> p c m", p=P)).then_inc(ld_ex, 16)
            upv = L0_ffn_up_w.rearrange("(m p) i -> m p i", p=PH)
            sp.dma_start(up_raw[:, :, 0:INT // 2], upv[:, :, 0:INT // 2]).then_inc(ld_up[0], 16)
            sp.dma_start(fc2[:], L0_ffn_fc2_w.rearrange("(c p) l -> p c l", p=P)).then_inc(ld_fc2, 16)
            sp.dma_start(fc_raw[:], L0_ffn_fc1_w.rearrange("(m p) i -> m p i", p=PH)).then_inc(ld_fc, 16)
            sp.dma_start(up_raw[:, :, INT // 2:INT], upv[:, :, INT // 2:INT]).then_inc(ld_up[1], 16)
            dnv = L0_ffn_down_w.rearrange("(c p) l -> p c l", p=P)
            for i in range(2):
                cs = slice(i * IC // 2, (i + 1) * IC // 2)
                sp.dma_start(dn_raw[:, cs, :], dnv[:, cs, :]).then_inc(ld_dn[i], 16)
            load_x(3)
            sp.dma_start(gamma[:], L0_ffn_ln_gamma.partition_broadcast(P)).then_inc(ld_gb, 16)
            sp.dma_start(rowb[:], L0_ffn_ln_beta.partition_broadcast(P)).then_inc(ld_gb, 16)
            for i, w in enumerate((L1_ffn_Wq, L1_ffn_Wk)):
                sp.dma_start(qk_raw[:, i], w.rearrange("(c p) l -> p c l", p=P)).then_inc(ld_qk, 16)
            sp.wait_ge(s_conv, TILES)
            sp.dma_start(w_raw, L1_ffn_W.rearrange("(c p) l -> p c l", p=P)).then_inc(ld_w, 16)
            sp.wait_ge(s_H, TILES)
            sp.dma_start(a_raw, L1_ffn_A.rearrange("e r l -> (e r) l")).then_inc(ld_ab, 16)
            bv = L1_ffn_Bm.rearrange("e (c p) r -> p c e r", p=P)
            for c in range(PH):
                sp.dma_start(b_raw[:, c], bv[:, c]).then_inc(ld_ab, 16)
            sp.wait_ge(s_xb, TILES)
            sp.dma_start(rowb[:], L1_ffn_b.partition_broadcast(P)).then_inc(ld_b, 16)
            for T in range(TILES):
                sp.wait_ge(s_fin, T + 1)
                sp.dma_start(out_dram[:, T, :], X[:, T, :]).then_inc(s_out, 16)
            sp.wait_ge(s_out, 16 * TILES)

        @block.gpsimd
        def _(pool):
            nc.gpsimd.memset(ident[:], 0.0).then_inc(s_ident, 1)
            nc.gpsimd.memset(wc_pad[:], 0.0).then_inc(s_zero, 1)
            pool.wait_ge(s_ident, 1)
            nc.gpsimd.affine_select(out=ident[:], in_=ident[:], compare_op=ALU.not_equal, fill=1.0, base=0,
                                    pattern=[[-1, P]], channel_multiplier=1).then_inc(s_ident, 1)
            nc.gpsimd.memset(gmask[:], 1.0).then_inc(s_gmask, 1)
            pool.wait_ge(s_gmask, 1)
            nc.gpsimd.affine_select(out=gmask[:], in_=gmask[:], compare_op=ALU.is_ge, fill=0.0, base=0,
                                    pattern=[[-CG, G]], channel_multiplier=1).then_inc(s_gmask, 1)
            pool.wait_ge(s_gmask, 2)
            nc.gpsimd.affine_select(out=gmask[:], in_=gmask[:], compare_op=ALU.is_ge, fill=0.0, base=CG - 1,
                                    pattern=[[CG, G]], channel_multiplier=-1).then_inc(s_gmask, 1)
            nc.gpsimd.memset(XS[:, :, 0:1], 0.0)
            nc.gpsimd.memset(XS[:, :, XW - 1:XW], 0.0).then_inc(s_zero, 1)
            nc.gpsimd.memset(nhalf[:], -0.5)
            nc.gpsimd.memset(BD[:], 0.0).then_inc(s_zero, 1)
            nc.gpsimd.memset(gate_hl[:].bitcast(mybir.dt.uint32), 0).then_inc(s_gatez, 1)
            pool.wait_ge(s_fch, 1)
            nc.gpsimd.tensor_tensor(fc_lo[:], fc_raw[:], fc_hi[:].bitcast(F32), ALU.subtract).then_inc(s_fc, 1)
            for c in range(IC):
                pool.wait_ge(s_dnh, c + 1)
                nc.gpsimd.tensor_tensor(dn_lo[:, c, :], dn_raw[:, c, :], dn_hi[:, c, :].bitcast(F32),
                                        ALU.subtract).then_inc(s_dn, 1)
            pool.wait_ge(ld_gb, 32)

            def add_beta(h):
                pool.wait_ge(xs_v, (3, 4)[h])
                pool.wait_ge(xs_a, (3, 4)[h])
                for t in range(TPH):
                    T = h * TPH + t
                    nc.gpsimd.tensor_tensor(X[:, T, :], X[:, T, :], rowb[:], ALU.add).then_inc(s_xb, 1)

            def norm_scale(T):
                t = T % TPH
                pool.wait_ge(s_mv, T + 1)
                if T >= TPH:
                    pool.wait_ge(s_x1, T - TPH + 1)
                nc.gpsimd.tensor_scalar(ve[:, t:t + 1], mv[:, t, 1:2], EPS, 1.0, ALU.add, ALU.mult)\
                    .then_inc(s_ve, 1)
                pool.wait_ge(s_ve, T + 1)
                nc.gpsimd.tensor_tensor(rstd[:, t:t + 1], ve[:, t:t + 1], nhalf[:], ALU.pow).then_inc(s_rstd, 1)

            def add_bias(h):
                for t in range(TPH):
                    T = h * TPH + t
                    pool.wait_ge(s_yp, T + 1)
                    nc.gpsimd.tensor_tensor(X[:, T, :], X[:, T, :], rowb[:], ALU.add).then_inc(s_x1b, 1)

            add_beta(0)
            add_beta(1)
            for T in range(TILES):
                norm_scale(T)
            pool.wait_ge(ld_b, 16)
            add_bias(0)
            add_bias(1)

        @block.scalar
        def _(act):
            act.dma_start(cw_nat[:], L0_cond_c_weight).then_inc(ld_c, 16)
            act.dma_start(wc_nat[:], L0_cond_weight).then_inc(ld_wc, 16)
            act.dma_start(fsb[:], fside_S_0.partition_broadcast(P)).then_inc(ld_fs, 16)
            act.dma_start(gate[:], L0_ffn_gate_w.rearrange("(m p) e -> m p e", p=PH)).then_inc(ld_gate, 16)

            def shift_copies(i):
                act.wait_ge(ld_x[i], 16)
                phase_copies(nc.scalar, *XPARTS[i]).then_inc(xs_a, 1)

            def split_up(c):
                act.wait_ge(ld_up[c // (IC // 2)], 16)
                nc.scalar.activation(up_hi[:, c], up_raw[:, :, c * P:(c + 1) * P], ACT.Copy).then_inc(s_uph, 1)

            def split_dn(c):
                act.wait_ge(ld_dn[c // (IC // 2)], 16)
                nc.scalar.activation(dn_hi[:, c, :], dn_raw[:, c, :], ACT.Copy).then_inc(s_dnh, 1)

            def split_H(T):
                t = T % TPH
                act.wait_ge(s_tf, T + 1)
                nc.scalar.activation(H_hi[:, :, t * P:(t + 1) * P], tf[:, T % 2], ACT.Copy).then_inc(s_Hh, 1)

            def up_relu(i):
                act.wait_ge(s_upp, i + 1)
                if i:
                    act.wait_ge(s_sq, i)
                else:
                    act.wait_ge(s_BD, 1)
                nc.scalar.activation(relu[:], U[i % 2], ACT.Relu).then_inc(s_relu, 1)

            def up_split(i):
                act.wait_ge(s_sq, i + 1)
                if i >= NR:
                    down_done(act, i - NR)
                nc.scalar.activation(R_hi[:, i % NR], U[i % 2], ACT.Copy).then_inc(s_Rh, 1)

            def scale_rows(h):
                act.wait_ge(s_sbp, h + 1)
                nc.scalar.activation(sbc[:], M[0], ACT.Copy).then_inc(s_sb, 1)

            def gate_copy(h):
                act.wait_ge(s_gT, h + 1)
                if h:
                    act.wait_ge(s_lats, LC)
                nc.scalar.activation(sbc[0:2 * NE, :], M[0][0:2 * NE, :], ACT.Copy).then_inc(s_gTs, 1)

            def lat_split(n):
                act.wait_ge(s_lats, n + 1)
                nc.scalar.activation(lat_hi[:, n % LC], M[(n + 1) % LC], ACT.Copy).then_inc(s_lath, 1)

            def group_split(g):
                act.wait_ge(s_wgp, g + 1)
                for dst, src in wg_dst(g, True):
                    last = nc.scalar.activation(dst, src, ACT.Copy)
                last.then_inc(s_wgh, 1)

            for i in range(3):
                shift_copies(i)
            act.wait_ge(ld_cond, 16 * 8)
            act.wait_ge(s_c1p, 1)
            nc.scalar.activation(h1[:], D[0][:, 0:N], ACT.Gelu, bias=b0[:, 0:1]).then_inc(s_c1, 1)
            split_up(0)
            split_H(0)
            act.wait_ge(s_c2p, 1)
            nc.scalar.activation(h2[:], D[1][:, 0:N], ACT.Gelu, bias=b1[:, 0:1]).then_inc(s_c2, 1)
            split_up(1)
            act.wait_ge(ld_fc, 16)
            nc.scalar.activation(fc_hi[:], fc_raw[:], ACT.Copy).then_inc(s_fch, 1)
            split_H(1)
            act.wait_ge(s_exTp, 1)
            nc.scalar.activation(exT[:].rearrange("p c m -> p (c m)"), D[2], ACT.Copy).then_inc(s_exT, 1)
            act.wait_ge(ld_gate, 16)
            act.wait_ge(s_gatez, 1)
            nc.scalar.activation(gate_hl[:, :, 0:NE], gate[:], ACT.Copy).then_inc(s_gateh, 1)
            act.wait_ge(s_att, 3)
            nc.scalar.activation(att[:, 2, :], att[:, 1, :], ACT.Exp, accum_out=att[:, 3, 0:1]).then_inc(s_aexp, 1)
            split_H(2)
            split_up(2)
            for i in range(LC):
                act.wait_ge(s_E2p, i + 1)
                nc.scalar.activation(ex_hi[:, i, :], (D[3], M[1])[i], ACT.Copy).then_inc(s_E2h, 1)
            split_H(3)
            act.wait_ge(s_aTp, 1)
            nc.scalar.activation(attT[:], D[0][0:KE, 0:N], ACT.Copy).then_inc(s_aT, 1)
            split_up(3)
            act.wait_ge(s_agg, 2)
            act.wait_ge(s_zero, 3)
            for b in range(2):
                ag = agg[:, b * (C // 2):(b + 1) * (C // 2), :].rearrange("p o (t s) -> p s t o", s=SPT)
                for s in range(SPT):
                    last = nc.scalar.activation(BD[C * s:C * (s + 1), :, C * s + b * (C // 2):C * s + (b + 1) * (C // 2)],
                                                ag[:, s], ACT.Copy)
            last.then_inc(s_BD, 1)
            for i in range(2):
                act.wait_ge(s_B1p, i + 1)
                nc.scalar.activation(B1[:, i * BANK:(i + 1) * BANK], D[2 + i], ACT.Copy).then_inc(s_B1, 1)

            for h in range(HALVES):
                i0 = h * IC
                if h:
                    for t in range(TPH):
                        split_H(TPH + t)
                        for g in conv_groups(t):
                            group_split(g)
                up_relu(i0)
                up_split(i0)
                if h == 0:
                    split_up(4)
                gate_copy(h)
                up_relu(i0 + 1)
                up_split(i0 + 1)
                if h == 0:
                    split_up(5)
                    split_dn(0)
                up_relu(i0 + 2)
                scale_rows(h)
                up_split(i0 + 2)
                for n in range(LC):
                    if h == 0:
                        split_dn(1 + n)
                        split_up(6 + n)
                    lat_split(h * LC + n)
                for c in range(3, IC):
                    if h:
                        group_split(GCONV + c - 3)
                    elif c < IC:
                        split_dn(c)
                    up_relu(i0 + c)
                    up_split(i0 + c)
                    if h == 0 and c == 3:
                        act.wait_ge(s_conv, TPH)
                        shift_copies(3)
                if h:
                    group_split(len(wgroups) - 1)

            def y_split(T):
                t = T % TPH
                act.wait_ge(s_yb, T + 1)
                nc.scalar.activation(H_hi[:, :, t * P:(t + 1) * P],
                                     mix_bank(T), ACT.Copy).then_inc(s_Yh, 1)

            def q_copy(T):
                act.wait_ge(s_qkp, T + 1)
                if T:
                    act.wait_ge(s_pr, T)
                nc.scalar.activation(qs[:], QK[T % 2][0][:, 0:QW], ACT.Copy).then_inc(s_q, 1)

            def exp_scores(T):
                act.wait_ge(s_nmx, T + 1)
                nc.scalar.activation(sm[:, T % 2, 2, :], sm[:, T % 2, 0, :], ACT.Exp, scale=SCALE,
                                     bias=sm[:, T % 2, 1, 1:2], accum_out=sm[:, T % 2, 3, 0:1]).then_inc(s_e, 1)

            def hw_split(T):
                act.wait_ge(s_hwp, T + 1)
                if T >= 2:
                    act.wait_ge(s_res, T - 1)
                nc.scalar.activation(hwT_hi[:, T % 2], QK[T % 2][0][:, 0:P], ACT.Copy).then_inc(s_hwh, 1)

            y_split(0)
            y_split(1)
            q_copy(0)
            exp_scores(0)
            y_split(2)
            for T in range(TILES):
                if T + 1 < TILES:
                    q_copy(T + 1)
                hw_split(T)
                if T + 1 < TILES:
                    exp_scores(T + 1)
                if T + 3 < TILES:
                    y_split(T + 3)

        @block.vector
        def _(dve):
            def shift_copies(i):
                dve.wait_ge(ld_x[i], 16)
                phase_copies(nc.vector, *XPARTS[i]).then_inc(xs_v, 1)

            def split_up(c):
                dve.wait_ge(s_uph, c + 1)
                nc.vector.tensor_tensor(up_lo[:, c], up_raw[:, :, c * P:(c + 1) * P], up_hi[:, c].bitcast(F32),
                                        ALU.subtract).then_inc(s_up, 1)

            def add_ctx(T):
                dve.wait_ge(s_conv, T + 1)
                dve.wait_ge(s_B0, 2)
                if T >= 2:
                    dve.wait_ge(s_H, T - 1)
                nc.vector.tensor_tensor(
                    tf[:, T % 2].rearrange("m p (n o) -> m n p o", o=C),
                    U[T % 2].rearrange("m (n p o) -> m n p o", n=SPT, p=PH),
                    B0[:, T * P:(T + 1) * P].rearrange("m (n o) -> m n o", o=C).unsqueeze(2)
                    .broadcast_to([P, SPT, PH, C]), ALU.add).then_inc(s_tf, 1)

            def split_H(T):
                t = T % TPH
                dve.wait_ge(s_Hh, T + 1)
                hs = slice(t * P, (t + 1) * P)
                nc.vector.tensor_tensor(H_lo[:, :, hs], tf[:, T % 2], H_hi[:, :, hs].bitcast(F32),
                                        ALU.subtract).then_inc(s_H, 1)

            def gate_sum(h):
                dve.wait_ge(s_gp, h + 1)
                for t in range(TPH):
                    last = nc.vector.max(top[:, t], M[1][:, t * NE:(t + 1) * NE])
                last.then_inc(s_top, 1)
                dve.wait_ge(s_top, h + 1)
                nc.vector.tensor_tensor(ssum[:].unsqueeze(2), top[:, :, 0:1], top[:, :, 1:2], ALU.add)\
                    .then_inc(s_sum, 1)
                dve.wait_ge(s_sum, h + 1)
                for t in range(TPH):
                    last = nc.vector.tensor_scalar(sbc[:, t * P:(t + 1) * P], ident[:], ssum[:, t:t + 1], None,
                                                   ALU.mult)
                last.then_inc(s_diag, 1)

            def up_square(i):
                dve.wait_ge(s_relu, i + 1)
                nc.vector.tensor_tensor(U[i % 2], U[i % 2], relu[:], ALU.mult).then_inc(s_sq, 1)

            def up_split(i):
                dve.wait_ge(s_Rh, i + 1)
                nc.vector.tensor_tensor(R_lo[:, i % NR], U[i % 2], R_hi[:, i % NR].bitcast(F32),
                                        ALU.subtract).then_inc(s_R, 1)

            def lat_scale(n):
                dve.wait_ge(s_latp, n + 1)
                dve.wait_ge(s_sb, n // LC + 1)
                b = M[(n + 1) % LC]
                nc.vector.tensor_tensor(b, b, sbc[:], ALU.mult).then_inc(s_lats, 1)

            def lat_split(n):
                dve.wait_ge(s_lath, n + 1)
                nc.vector.tensor_tensor(lat_lo[:, n % LC], M[(n + 1) % LC], lat_hi[:, n % LC].bitcast(F32),
                                        ALU.subtract).then_inc(s_lat, 1)

            def group_split(g):
                dve.wait_ge(s_wgh, g + 1)
                for (lo, src), (hi, _) in zip(wg_dst(g, False), wg_dst(g, True)):
                    last = nc.vector.tensor_tensor(lo, src, hi.bitcast(F32), ALU.subtract)
                last.then_inc(s_wg, 1)

            def norm_stats(T):
                dve.wait_ge(s_ffn, T + 1)
                nc.vector.bn_stats(st6[:, T % 2], D[T % TPH]).then_inc(s_bn, 1)
                dve.wait_ge(s_bn, T + 1)
                if T >= TPH:
                    dve.wait_ge(s_ve, T - TPH + 1)
                nc.vector.bn_aggr(mv[:, T % TPH], st6[:, T % 2]).then_inc(s_mv, 1)
                dve.wait_ge(s_mv, T + 1)
                if T == 0:
                    dve.wait_ge(ld_gb, 32)
                nc.vector.scalar_tensor_tensor(D[T % TPH], D[T % TPH], mv[:, T % TPH, 0:1], gamma[:],
                                               ALU.subtract, ALU.mult).then_inc(s_cen, 1)

            def norm_apply(T):
                dve.wait_ge(s_rstd, T + 1)
                dve.wait_ge(s_cen, T + 1)
                dve.wait_ge(s_xb, T + 1)
                nc.vector.scalar_tensor_tensor(X[:, T, :], D[T % TPH], rstd[:, T % TPH:T % TPH + 1], X[:, T, :],
                                               ALU.mult, ALU.add).then_inc(s_x1, 1)

            nc.vector.memset(ones[:], 1.0).then_inc(s_ones, 1)
            dve.wait_ge(s_cTp, 1)
            nc.vector.tensor_copy(cT[:], M[0][:, 0:N]).then_inc(s_cT, 1)
            dve.wait_ge(s_cT, 1)
            nc.vector.tensor_tensor(prod0[:], bcast_mid(M[0][:, N:N + C], N),
                                    cT[:].unsqueeze(2).broadcast_to([CD, N, C]), ALU.mult).then_inc(s_prod0, 1)
            dve.wait_ge(ld_wc, 16)
            dve.wait_ge(s_zero, 1)
            dve.wait_ge(s_gmask, 3)
            nc.vector.tensor_tensor(
                wc_pad[:, PH - 1:PH - 1 + KT, :].rearrange("p k (g i) -> p k g i", g=G),
                wc_nat[:].rearrange("p i k -> p k i").unsqueeze(2).broadcast_to([C, KT, G, CG]),
                gmask[:].unsqueeze(1).unsqueeze(3).broadcast_to([C, KT, G, CG]), ALU.mult).then_inc(s_wcp, 1)
            shift_copies(0)
            dve.wait_ge(s_wcT, 1)
            nc.vector.tensor_copy(wconv[:].rearrange("p a q -> p (a q)"), M[1][:, 0:NWIN * P]).then_inc(s_wconv, 1)
            shift_copies(1)
            shift_copies(2)
            dve.wait_ge(ld_fs, 16)
            for i in range(2):
                dve.wait_ge(s_B0p, i + 1)
                nc.vector.tensor_tensor(B0[:, i * BANK:(i + 1) * BANK].rearrange("p (n o) -> p n o", o=C),
                                        D[i].rearrange("p (n o) -> p n o", o=C), bcast_mid(fsb[:], BANK // C),
                                        ALU.add).then_inc(s_B0, 1)
            add_ctx(0)
            split_up(0)
            split_H(0)
            add_ctx(1)
            split_up(1)
            split_H(1)
            dve.wait_ge(s_lgp, 1)
            nc.vector.tensor_tensor(att[:, 0, :], D[0][0:N, 0:KE], b2[:], ALU.add).then_inc(s_att, 1)
            dve.wait_ge(s_att, 1)
            nc.vector.reduce_max(att[:, 3, 1:2], att[:, 0, :], AX_X).then_inc(s_att, 1)
            dve.wait_ge(s_att, 2)
            nc.vector.tensor_scalar(att[:, 1, :], att[:, 0, :], att[:, 3, 1:2], None, ALU.subtract).then_inc(s_att, 1)
            add_ctx(2)
            dve.wait_ge(s_aexp, 1)
            nc.vector.reciprocal(att[:, 3, 2:3], att[:, 3, 0:1]).then_inc(s_att, 1)
            dve.wait_ge(s_att, 4)
            nc.vector.tensor_scalar(att[:, 0, :], att[:, 2, :], att[:, 3, 2:3], None, ALU.mult).then_inc(s_att, 1)
            split_H(2)
            split_up(2)
            dve.wait_ge(s_gateh, 1)
            nc.vector.tensor_tensor(gate_hl[:, :, NE:2 * NE], gate[:], gate_hl[:, :, 0:NE].bitcast(F32),
                                    ALU.subtract).then_inc(s_gate, 1)
            nc.vector.tensor_tensor(fold[:], ident[0:2 * NE, 0:NE], ident[0:2 * NE, NE:2 * NE], ALU.add)\
                .then_inc(s_fold, 1)
            for i in range(LC):
                dve.wait_ge(s_E2h, i + 1)
                nc.vector.tensor_tensor(ex_lo[:, i, :], (D[3], M[1])[i], ex_hi[:, i, :].bitcast(F32),
                                        ALU.subtract).then_inc(s_E2, 1)
            add_ctx(3)
            split_H(3)
            dve.wait_ge(s_aT, 1)
            nc.vector.tensor_tensor(prod1[:], bcast_mid(bk[:], N), attT[:].unsqueeze(2).broadcast_to([KE, N, C]),
                                    ALU.mult).then_inc(s_prod1, 1)
            split_up(3)
            dve.wait_ge(s_AGp, 1)
            for b in range(2):
                nc.vector.transpose(agg[:, b * (C // 2):(b + 1) * (C // 2), :].rearrange("i o n -> i (o n)"),
                                    D[b][0:C, :]).then_inc(s_agg, 1)
            for h in range(HALVES):
                i0 = h * IC
                if h:
                    for t in range(TPH):
                        add_ctx(TPH + t)
                        if t < 2:
                            norm_stats(t)
                        split_H(TPH + t)
                        if t < 2:
                            norm_apply(t)
                        for g in conv_groups(t):
                            group_split(g)
                up_square(i0)
                up_split(i0)
                if h == 0:
                    split_up(4)
                gate_sum(h)
                up_square(i0 + 1)
                up_split(i0 + 1)
                if h == 0:
                    split_up(5)
                else:
                    norm_stats(2)
                up_square(i0 + 2)
                up_split(i0 + 2)
                if h:
                    norm_apply(2)
                    norm_stats(3)
                for n in range(LC):
                    if h == 0:
                        split_up(6 + n)
                    lat_scale(h * LC + n)
                    lat_split(h * LC + n)
                    if h and n == 0:
                        norm_apply(3)
                for c in range(3, IC):
                    if h:
                        group_split(GCONV + c - 3)
                    up_square(i0 + c)
                    up_split(i0 + c)
                    if h == 0 and c == 3:
                        shift_copies(3)
                if h:
                    group_split(len(wgroups) - 1)

            def y_bias(T):
                dve.wait_ge(s_yp, T + 1)
                b = mix_bank(T)
                nc.vector.tensor_tensor(b, b, bcast_mid(B1[:, T * P:(T + 1) * P], PH), ALU.add).then_inc(s_yb, 1)

            def y_split(T):
                hs = slice(T % TPH * P, (T % TPH + 1) * P)
                dve.wait_ge(s_Yh, T + 1)
                nc.vector.tensor_tensor(H_lo[:, :, hs], mix_bank(T), H_hi[:, :, hs].bitcast(F32), ALU.subtract).then_inc(s_Y, 1)

            def scores(T):
                s = sm[:, T % 2]
                dve.wait_ge(s_q, T + 1)
                nc.vector.tensor_tensor(pr[:], QK[T % 2][1][:, 0:QW], qs[:], ALU.mult).then_inc(s_pr, 1)
                dve.wait_ge(s_pr, T + 1)
                nc.vector.reduce_sum(s[:, 0, :], pr[:].rearrange("p (e d) -> p e d", e=E), AX_X).then_inc(s_sc, 1)
                dve.wait_ge(s_sc, T + 1)
                nc.vector.reduce_max(s[:, 1, 0:1], s[:, 0, :], AX_X).then_inc(s_mx, 1)
                dve.wait_ge(s_mx, T + 1)
                nc.vector.tensor_scalar(s[:, 1, 1:2], s[:, 1, 0:1], -SCALE, None, ALU.mult).then_inc(s_nmx, 1)

            def weigh(T):
                s = sm[:, T % 2]
                dve.wait_ge(s_e, T + 1)
                nc.vector.reciprocal(s[:, 3, 1:2], s[:, 3, 0:1]).then_inc(s_rc, 1)
                dve.wait_ge(s_rc, T + 1)
                if T:
                    dve.wait_ge(s_hwp, T)
                for a in range(2):
                    last = nc.vector.scalar_tensor_tensor(
                        hw[:, a * HH:(a + 1) * HH].rearrange("p (e r) -> p e r", e=EH),
                        QK[T % 2][a][:, QW:QKW].rearrange("p (e r) -> p e r", e=EH), s[:, 3, 1:2],
                        s[:, 2, a * EH:(a + 1) * EH].unsqueeze(2).broadcast_to([P, EH, R]), ALU.mult, ALU.mult)
                last.then_inc(s_hw, 1)

            def hw_split(T):
                dve.wait_ge(s_hwh, T + 1)
                nc.vector.tensor_tensor(hwT_lo[:, T % 2], QK[T % 2][0][:, 0:P], hwT_hi[:, T % 2].bitcast(F32),
                                        ALU.subtract).then_inc(s_hwT, 1)

            def finish(T):
                dve.wait_ge(s_res, T + 1)
                dve.wait_ge(s_x1b, T + 1)
                nc.vector.tensor_tensor(X[:, T, :], D[T % TPH], X[:, T, :], ALU.add).then_inc(s_fin, 1)

            y_bias(0)
            y_split(0)
            norm_stats(TPH)
            y_bias(1)
            y_split(1)
            norm_apply(TPH)
            norm_stats(TPH + 1)
            norm_stats(TPH + 2)
            norm_apply(TPH + 1)
            norm_apply(TPH + 2)
            scores(0)
            norm_stats(TPH + 3)
            weigh(0)
            norm_apply(TPH + 3)
            y_bias(2)
            y_split(2)
            for T in range(TILES):
                if T + 1 < TILES:
                    scores(T + 1)
                hw_split(T)
                if T + 1 < TILES:
                    weigh(T + 1)
                finish(T)
                if T + 3 < TILES:
                    y_bias(T + 3)
                    y_split(T + 3)

        @block.tensor
        def _(pe):
            def mm3(o, lh, ll, rh, rl, start, stop):
                nc.tensor.matmul(o, lh, rh, start=start, stop=False)
                nc.tensor.matmul(o, lh, rl, start=False, stop=False)
                return nc.tensor.matmul(o, ll, rh, start=False, stop=stop)

            def conv(T):
                if T >= 2:
                    pe.wait_ge(s_tf, T - 1)
                if T >= TPH:
                    pe.wait_ge(s_R, IC)
                for s in range(SPT):
                    for a in range(NWIN):
                        last = nc.tensor.matmul(U[T % 2][:, s * P:(s + 1) * P],
                                                XS[:, T % TPH * SPT + s, a:a + P], wconv[:, a],
                                                start=(a == 0), stop=(a == NWIN - 1))
                last.then_inc(s_conv, 1)

            def gate_rows(h):
                if h == 0:
                    pe.wait_ge(s_gate, 1)
                    pe.wait_ge(s_fold, 1)
                else:
                    pe.wait_ge(s_wg, GCONV - 1)
                for p in range(PH):
                    nc.tensor.matmul(M[0], gate_hl[:, p], H_hi[:, p], start=(p == 0), stop=False)
                    last = nc.tensor.matmul(M[0], gate_hl[:, p], H_lo[:, p], start=False, stop=(p == PH - 1))
                last.then_inc(s_gT, 1)

            def gate_logits(h):
                pe.wait_ge(s_gTs, h + 1)
                if h == 0:
                    pe.wait_ge(s_E2, 2)
                else:
                    pe.wait_ge(s_wg, GCONV)
                for t in range(TPH):
                    last = nc.tensor.matmul(M[1][:, t * NE:(t + 1) * NE], sbc[0:2 * NE, t * P:(t + 1) * P],
                                            fold[:], start=True, stop=True)
                last.then_inc(s_gp, 1)

            def up(i, part=None):
                h, c = divmod(i, IC)
                if h == 0:
                    pe.wait_ge(s_up, c + 1)
                if part is None:
                    part = slice(0, TOKH)
                if c < 2:
                    pe.wait_ge(s_H, TPH * h + part.stop // P)
                    pe.wait_ge(s_tf, TPH * h + 3 + c)
                if i >= 2:
                    pe.wait_ge(s_R, i - 1)
                for p in range(PH):
                    last = mm3(U[i % 2][:, part], up_hi[:, c, p], up_lo[:, c, p], H_hi[:, p, part],
                               H_lo[:, p, part], p == 0, p == PH - 1)
                if part.stop == TOKH:
                    last.then_inc(s_upp, 1)

            def scale_rows(h):
                pe.wait_ge(s_diag, h + 1)
                for t in range(TPH):
                    last = nc.tensor.matmul(M[0][:, t * P:(t + 1) * P], ones[:], sbc[:, t * P:(t + 1) * P],
                                            start=True, stop=True)
                last.then_inc(s_sbp, 1)

            def latent(n):
                h, c = divmod(n, LC)
                if c == 0:
                    pe.wait_ge(s_top, h + 1)
                else:
                    pe.wait_ge(s_sb, h + 1)
                if h == 0:
                    pe.wait_ge(s_fc, 1)
                for p in range(PH):
                    last = mm3(M[(n + 1) % LC], fc_hi[:, p, c * P:(c + 1) * P], fc_lo[:, p, c * P:(c + 1) * P],
                               H_hi[:, p], H_lo[:, p], p == 0, p == PH - 1)
                last.then_inc(s_latp, 1)

            def down(i):
                h, c = divmod(i, IC)
                pe.wait_ge(s_R, i + 1)
                if h == 0:
                    pe.wait_ge(s_dn, c + 1)
                for t in range(TPH):
                    if h and c == 0:
                        pe.wait_ge(s_x1, t + 1)
                    if h == 0 and c == 0:
                        pe.wait_ge(s_BD, 1)
                        pe.wait_ge(s_B1, 2)
                        pe.wait_ge(s_E2, 2)
                    ts = slice(t * P, (t + 1) * P)
                    last = mm3(D[t], R_hi[:, i % NR, ts], R_lo[:, i % NR, ts], dn_hi[:, c], dn_lo[:, c],
                               c == 0, c == IC - 1)
                    if c == IC - 1:
                        last.then_inc(s_ffn, 1)
                    elif t == TPH - 1:
                        last.then_inc(s_down, 1)

            def routed(h):
                pe.wait_ge(s_lat, LC * (h + 1))
                for t in range(TPH):
                    ts = slice(t * P, (t + 1) * P)
                    for c in range(LC):
                        mm3(D[t], lat_hi[:, c, ts], lat_lo[:, c, ts], ex_hi[:, c], ex_lo[:, c], False, False)

            def turn_group(g):
                what, p = wgroups[g]
                if g >= 2:
                    pe.wait_ge(s_wg, g - 1)
                if g == GCONV:
                    pe.wait_ge(s_lat, LC * HALVES)
                if what == "w" and p == 0:
                    pe.wait_ge(ld_w, 16)
                if what == "a":
                    pe.wait_ge(ld_ab, 16 * (1 + PH))
                if what == "qk" and p == 0:
                    pe.wait_ge(ld_qk, 32)
                ps = slice(p * P, (p + 1) * P)
                src = {
                    "w": lambda k: w_raw[:, k, ps],
                    "qk": lambda k: qk_raw[:, k // LC, k % LC, ps],
                    "a": lambda k: a_raw[:, k * P:(k + 1) * P],
                    "b": lambda k: b_raw[:, k].rearrange("p e r -> p (e r)"),
                }[what]
                for k in range(PH):
                    last = nc.tensor.transpose(M[g % 2][:, k * P:(k + 1) * P], src(k), ident[:])
                last.then_inc(s_wgp, 1)

            def mix(T):
                pe.wait_ge(s_x1, T + 1)
                if T < 2:
                    pe.wait_ge(s_wg, len(wgroups) - 1 + T)
                elif T < TPH:
                    pe.wait_ge(s_x1, TPH + T + 1)
                else:
                    pe.wait_ge(s_fin, T - TPH + 1)
                for p in range(PH):
                    last = nc.tensor.matmul(mix_bank(T)[:, p, :], X[:, T, p * P:(p + 1) * P], BD[:, T],
                                            start=True, stop=True)
                last.then_inc(s_yp, 1)

            def qk(T):
                ts = slice(T % TPH * P, (T % TPH + 1) * P)
                pe.wait_ge(s_Y, T + 1)
                if T >= 2:
                    pe.wait_ge(s_hwT, T - 1)
                for a in range(2):
                    for p in range(PH):
                        last = mm3(QK[T % 2][a][:, 0:QKW], H_hi[:, p, ts], H_lo[:, p, ts],
                                   qkT_hi[:, p, a], qkT_lo[:, p, a], p == 0, p == PH - 1)
                last.then_inc(s_qkp, 1)

            def dense(T):
                ts = slice(T % TPH * P, (T % TPH + 1) * P)
                if T < 2:
                    pe.wait_ge(s_x1, TPH + T + 1)
                for p in range(PH):
                    mm3(D[T % TPH], H_hi[:, p, ts], H_lo[:, p, ts], wT_hi[:, p], wT_lo[:, p], p == 0, False)

            def turn_hw(T):
                pe.wait_ge(s_hw, T + 1)
                nc.tensor.transpose(QK[T % 2][0][:, 0:P], hw[:], ident[:]).then_inc(s_hwp, 1)

            def combine(T):
                pe.wait_ge(s_hwT, T + 1)
                mm3(D[T % TPH], hwT_hi[:, T % 2], hwT_lo[:, T % 2], bT_hi[:], bT_lo[:], False, True)\
                    .then_inc(s_res, 1)

            pe.wait_ge(s_ident, 2)
            pe.wait_ge(ld_c, 32)
            nc.tensor.transpose(M[0][:, 0:N], c_nat[:], ident[0:N, 0:N])
            nc.tensor.transpose(M[0][:, N:N + C], cw_nat[:], ident[0:C, 0:C]).then_inc(s_cTp, 1)
            pe.wait_ge(s_wcp, 1)
            for a in range(NWIN):
                for p in range(PH):
                    k0 = PH - 1 + PH * a - p
                    last = nc.tensor.transpose(M[1][:, a * P + p * C:a * P + (p + 1) * C],
                                               wc_pad[:, k0:k0 + PH, :].rearrange("p k c -> p (k c)"),
                                               ident[0:C, 0:C])
            last.then_inc(s_wcT, 1)
            pe.wait_ge(s_wconv, 1)
            pe.wait_ge(s_zero, 2)
            pe.wait_ge(xs_v, 1)
            pe.wait_ge(xs_a, 1)
            conv(0)
            pe.wait_ge(s_ones, 1)
            pe.wait_ge(s_prod0, 1)
            pf = prod0[:].rearrange("d n o -> d (n o)")
            for i in range(2):
                nc.tensor.matmul(D[i], ones[:], pf[:, i * BANK:(i + 1) * BANK], start=True, stop=True)\
                    .then_inc(s_B0p, 1)
            pe.wait_ge(xs_v, 2)
            pe.wait_ge(xs_a, 2)
            conv(1)
            pe.wait_ge(ld_cond, 16 * 8)
            pe.wait_ge(s_B0, 1)
            nc.tensor.matmul(D[0][:, 0:N], W0[:], cT[:], start=True, stop=True).then_inc(s_c1p, 1)
            pe.wait_ge(ld_ex, 16)
            for mc in range(LC):
                for lc in range(LC):
                    last = nc.tensor.transpose(D[2][:, mc * LAT + lc * P:mc * LAT + (lc + 1) * P],
                                               exraw[:, lc, mc * P:(mc + 1) * P], ident[:])
            last.then_inc(s_exTp, 1)
            pe.wait_ge(xs_v, 3)
            pe.wait_ge(xs_a, 3)
            conv(2)
            pe.wait_ge(s_c1, 1)
            pe.wait_ge(s_B0, 2)
            nc.tensor.matmul(D[1][:, 0:N], W1[:], h1[:], start=True, stop=True).then_inc(s_c2p, 1)
            conv(3)
            pe.wait_ge(s_c2, 1)
            nc.tensor.matmul(D[0][0:N, 0:KE], h2[:], W2[:], start=True, stop=True).then_inc(s_lgp, 1)
            pe.wait_ge(s_exT, 1)
            pe.wait_ge(ld_fc2, 16)
            for lc in range(LC):
                for mc in range(LC):
                    last = nc.tensor.matmul((D[3], M[1])[lc], exT[:, mc, lc * P:(lc + 1) * P], fc2[:, mc],
                                            start=(mc == 0), stop=(mc == LC - 1))
                last.then_inc(s_E2p, 1)
            pe.wait_ge(s_att, 5)
            nc.tensor.transpose(D[0][0:KE, 0:N], att[:, 0, :], ident[0:N, 0:N]).then_inc(s_aTp, 1)

            def mixing():
                pe.wait_ge(s_aT, 1)
                wf = wk[:].rearrange("k o i -> k (o i)")
                for b in range(2):
                    last = nc.tensor.matmul(D[b][0:N, :], attT[:], wf[:, b * BANK:(b + 1) * BANK],
                                            start=True, stop=True)
                last.then_inc(s_AGp, 1)
                pe.wait_ge(s_prod1, 1)
                pf1 = prod1[:].rearrange("k n o -> k (n o)")
                for i in range(2):
                    if i:
                        pe.wait_ge(s_E2, 1)
                    nc.tensor.matmul(D[2 + i], ones[0:KE, :], pf1[:, i * BANK:(i + 1) * BANK],
                                     start=True, stop=True).then_inc(s_B1p, 1)

            for h in range(HALVES):
                if h:
                    pe.wait_ge(xs_v, 4)
                    pe.wait_ge(xs_a, 4)
                    for t in range(TPH):
                        conv(TPH + t)
                        for g in conv_groups(t):
                            turn_group(g)
                for i in (h * IC, h * IC + 1):
                    up(i, slice(0, TOKH // 2))
                if h == 0:
                    mixing()
                up(h * IC, slice(TOKH // 2, TOKH))
                gate_rows(h)
                up(h * IC + 1, slice(TOKH // 2, TOKH))
                gate_logits(h)
                up(h * IC + 2)
                scale_rows(h)
                for n in range(LC):
                    latent(h * LC + n)
                for c in range(IC):
                    down(h * IC + c)
                    if c == 0:
                        routed(h)
                    if c + 3 < IC:
                        up(h * IC + c + 3)
                    if h and c < IC - 2:
                        turn_group(GCONV + c)
                    if h and c >= IC - 2:
                        mix(c - IC + 2)

            qk(0)
            for T in range(TILES):
                if T + 1 < TILES:
                    qk(T + 1)
                if T == 0:
                    mix(2)
                turn_hw(T)
                dense(T)
                combine(T)
                if T + 3 < TILES:
                    mix(T + 3)


_INS = ['x', 'cond_128', 'fside_S_0', 'L0_cond_weight', 'L0_cond_c_weight', 'L0_ffn_gate_w', 'L0_ffn_up_w',
        'L0_ffn_down_w', 'L0_ffn_fc1_w', 'L0_ffn_fc2_w', 'L0_ffn_expert_w', 'L0_ffn_ln_gamma', 'L0_ffn_ln_beta',
        'L1_cond_W0', 'L1_cond_b0', 'L1_cond_W1', 'L1_cond_b1', 'L1_cond_W2', 'L1_cond_b2', 'L1_cond_weight',
        'L1_cond_bias_k', 'L1_ffn_W', 'L1_ffn_b', 'L1_ffn_Wq', 'L1_ffn_Wk', 'L1_ffn_A', 'L1_ffn_Bm']
_OUTS = [((32, 32, 512), 'float32')]


def kernel(**inputs):
    import numpy as _np
    import concourse.bacc as _bacc
    from concourse import mybir as _mybir
    from concourse.bass_utils import run_bass_kernel_spmd as _run

    nc = _bacc.Bacc("TRN2", target_bir_lowering=False, num_devices=1, dynamic_dma_scratch_size=1024)
    arrays, args = {}, []
    for name in _INS:
        a = _np.ascontiguousarray(inputs[name])
        arrays[f"in_{name}_dram"] = a
        args.append(nc.dram_tensor(f"in_{name}_dram", a.shape, _mybir.dt.from_np(a.dtype), kind="ExternalInput").ap())
    for i, (shape, dtype) in enumerate(_OUTS):
        dt = _mybir.dt.from_np(_np.dtype(dtype))
        args.append(nc.dram_tensor(f"out_{i}_dram", shape, dt, kind="ExternalOutput").ap())
    bass_adaln_ffn(nc, *args)
    r = _run(nc, [arrays], core_ids=[0])
    got = tuple(r.results[0][f"out_{i}_dram"] for i in range(len(_OUTS)))
    return got[0]
```

```python
import math
from contextlib import ExitStack

import concourse.bass as bass
from concourse import mybir

F32 = mybir.dt.float32
F32R = mybir.dt.float32r
ALU = mybir.AluOpType
ACT = mybir.ActivationFunctionType
AX_X = mybir.AxisListType.X

P = 128
BANK = 512


def bass_adaln_ffn(
    nc: bass.Bass,
    x: bass.AP,
    cond_128: bass.AP,
    fside_S_0: bass.AP,
    L0_cond_weight: bass.AP,
    L0_cond_c_weight: bass.AP,
    L0_ffn_gate_w: bass.AP,
    L0_ffn_up_w: bass.AP,
    L0_ffn_down_w: bass.AP,
    L0_ffn_fc1_w: bass.AP,
    L0_ffn_fc2_w: bass.AP,
    L0_ffn_expert_w: bass.AP,
    L0_ffn_ln_gamma: bass.AP,
    L0_ffn_ln_beta: bass.AP,
    L1_cond_W0: bass.AP,
    L1_cond_b0: bass.AP,
    L1_cond_W1: bass.AP,
    L1_cond_b1: bass.AP,
    L1_cond_W2: bass.AP,
    L1_cond_b2: bass.AP,
    L1_cond_weight: bass.AP,
    L1_cond_bias_k: bass.AP,
    L1_ffn_W: bass.AP,
    L1_ffn_b: bass.AP,
    L1_ffn_Wq: bass.AP,
    L1_ffn_Wk: bass.AP,
    L1_ffn_A: bass.AP,
    L1_ffn_Bm: bass.AP,
    out: bass.AP,
):
    N, C, L = x.shape
    CD = cond_128.shape[1]
    INT = L0_ffn_up_w.shape[1]
    LAT = L0_ffn_fc1_w.shape[1]
    NE = L0_ffn_gate_w.shape[1]
    KT = L0_cond_weight.shape[2]
    CG = L0_cond_weight.shape[1]
    KE, CHID = L1_cond_W2.shape[1], L1_cond_W0.shape[1]
    E, R, _ = L1_ffn_A.shape
    DK = L1_ffn_Wq.shape[0] // E
    EPS = 1e-5

    SPT = P // C
    TILES = N // SPT
    HALVES = 2
    TPH = TILES // HALVES
    NPH = N // HALVES
    TOKH = TPH * P
    PH = L // P
    IC = INT // P
    LC = LAT // P
    G = C // CG
    QW = E * DK
    HH = E * R // 2
    EH = E // 2
    QKW = QW + HH
    NWIN = 3
    XW = P + 2
    NR = 3
    SCALE = 1.0 / math.sqrt(DK)
    assert L == BANK and TOKH == BANK and PH == 4 and C == 32 and KT == 9 and 2 * QKW == 640

    xt_dram = x.rearrange("(t s) c l -> (s c) t l", s=SPT)
    out_dram = out.rearrange("(t s) c l -> (s c) t l", s=SPT)

    with ExitStack() as ctx:
        def sb(name, shape, dt=F32, scope=ctx):
            return scope.enter_context(nc.sbuf_tensor(name, shape, dt))

        def sem(name):
            return ctx.enter_context(nc.semaphore(name))

        PS = ctx.enter_context(nc.psum_tensor("PS", [P, 8, BANK], F32))
        D = [PS[:, b, :] for b in range(4)]
        U = [PS[:, 4, :], PS[:, 5, :]]
        M = [PS[:, 6, :], PS[:, 7, :]]
        QK = [(U[0], U[1]), (M[0], M[1])]

        ident = sb("ident", [P, P])
        ones_r = sb("ones_r", [P, P], F32R)
        ones = sb("ones", [P, P])
        X = sb("X", [P, TILES, L])
        XS = sb("XS", [P, NPH, XW])
        wconv = sb("wconv", [P, NWIN, P])
        up_hi = sb("up_hi", [P, IC, PH, P], F32R)
        up_lo = sb("up_lo", [P, IC, PH, P], F32R)
        dn_hi = sb("dn_hi", [P, IC, L], F32R)
        dn_lo = sb("dn_lo", [P, IC, L], F32R)
        fc_hi = sb("fc_hi", [P, PH, LAT], F32R)
        fc_lo = sb("fc_lo", [P, PH, LAT], F32R)
        ex_hi = sb("ex_hi", [P, LC, L], F32R)
        ex_lo = sb("ex_lo", [P, LC, L], F32R)
        gate = sb("gate", [P, PH, NE])
        gate_hl = sb("gate_hl", [P, PH, P], F32R)
        logit = sb("logit", [P, TPH, NE])
        gamma = sb("gamma", [P, L])
        rowb = sb("rowb", [P, L])
        B0 = sb("B0", [P, N * C])
        B1 = sb("B1", [P, N * C])
        BD = sb("BD", [P, TILES, P])
        H_hi = sb("H_hi", [P, PH, TOKH], F32R)
        H_lo = sb("H_lo", [P, PH, TOKH], F32R)
        tf = sb("tf", [P, 2, PH, P])
        sbc = sb("sbc", [P, TOKH])
        top = sb("top", [P, TPH, 8])
        ssum = sb("ssum", [P, TPH])
        ssum_hi = sb("ssum_hi", [P, TPH], F32R)
        ssum_lo = sb("ssum_lo", [P, TPH], F32R)
        st6 = sb("st6", [P, 2, 6])
        mv = sb("mv", [P, TPH, 2])
        ve = sb("ve", [P, TPH])
        nhalf = sb("nhalf", [P, 1])
        rstd = sb("rstd", [P, TPH])
        qk_raw = sb("qk_raw", [P, PH, 2, QW])
        qs = sb("qs", [P, QW])
        pr = sb("pr", [P, QW])
        hw = sb("hw", [P, P])
        hwT_hi = sb("hwT_hi", [P, 2, P], F32R)
        hwT_lo = sb("hwT_lo", [P, 2, P], F32R)
        sm = sb("sm", [P, 2, 4, E])

        with ExitStack() as early:
            def se(name, shape):
                return sb(name, shape, F32, early)
            c_nat = se("c_nat", [N, CD])
            cw_nat = se("cw_nat", [C, CD])
            cT = se("cT", [CD, N])
            cwT = se("cwT", [CD, C])
            fsb = se("fsb", [P, C])
            wc_nat = se("wc_nat", [C, CG, KT])
            wc_pad = se("wc_pad", [C, NWIN * PH + PH - 1, C])
            gmask = se("gmask", [C, G])
            exraw = se("exraw", [P, LC, LAT])
            W0 = se("W0", [CD, CHID])
            W1 = se("W1", [CHID, CHID])
            W2 = se("W2", [CHID, KE])
            b0 = se("b0", [CHID, 1])
            b1 = se("b1", [CHID, 1])
            b2 = se("b2", [N, KE])
            h1 = se("h1", [CHID, N])
            h2 = se("h2", [CHID, N])
            att = se("att", [N, 4, KE])
            attT = se("attT", [KE, N])
            bk = se("bk", [KE, C])
        relu = sb("relu", [P, TOKH])
        ring = sb("ring", [P, NR - 1, 2, TOKH], F32R)
        with ExitStack() as later:
            wk = sb("wk", [KE, C, C], F32, later)
            prod1 = sb("prod1", [KE, N, C], F32, later)
            prod0 = sb("prod0", [CD, N, C], F32, later)
            agg = prod0[0:C]
        ring_last = sb("ring_last", [P, 2, TOKH], F32R)
        R_hi = [ring[:, 0, 0], ring[:, 1, 0], ring_last[:, 0]]
        R_lo = [ring[:, 0, 1], ring[:, 1, 1], ring_last[:, 1]]
        lat_hi = sb("lat_hi", [P, LC, TOKH], F32R)
        lat_lo = sb("lat_lo", [P, LC, TOKH], F32R)
        diag_hi, diag_lo = lat_hi[:, 0], lat_hi[:, 1]

        with ExitStack() as raw:
            up_raw = sb("up_raw", [P, PH, INT], F32, raw)
            dn_raw = sb("dn_raw", [P, IC, L], F32, raw)
            fc_raw = sb("fc_raw", [P, PH, LAT], F32, raw)
            fc2 = sb("fc2", [P, LC, L], F32, raw)
        qkT_hi = sb("qkT_hi", [P, PH, 2, QKW], F32R)
        qkT_lo = sb("qkT_lo", [P, PH, 2, QKW], F32R)
        wT_hi = sb("wT_hi", [P, PH, L], F32R)
        wT_lo = sb("wT_lo", [P, PH, L], F32R)
        bT_hi = sb("bT_hi", [P, L], F32R)
        bT_lo = sb("bT_lo", [P, L], F32R)

        w_raw = XS[:].rearrange("p n w -> p (n w)")[:, 0:PH * L].rearrange("p (c l) -> p c l", c=PH)
        tflat = tf[:].rearrange("p a b c -> p (a b c)")
        a_raw = tflat[:, 0:L].rearrange("p (c q) -> p c q", c=PH)
        b_raw = tflat[:, L:2 * L]

        prod0_hi, prod0_lo = (t[:, 0:2, :].rearrange("p a b -> p (a b)") for t in (H_hi, H_lo))
        prod1_hi, prod1_lo = (dn_lo[0:KE, i:i + 2, :].rearrange("p a b -> p (a b)") for i in (4, 6))
        fc2_hi, fc2_lo = dn_lo[:, 4:6, :], dn_lo[:, 6:8, :]
        exT_hi, exT_lo = (t.rearrange("p (c m) -> p c m", c=LC) for t in (ex_lo[:, 0, :], ex_lo[:, 1, :]))

        ld_c = sem("ld_c")
        ld_fs = sem("ld_fs")
        ld_wc = sem("ld_wc")
        ld_x = [sem(f"ld_x{i}") for i in range(4)]
        ld_ex = sem("ld_ex")
        ld_fc2 = sem("ld_fc2")
        ld_up = [sem(f"ld_up{i}") for i in range(2)]
        ld_fc = sem("ld_fc")
        ld_gate = sem("ld_gate")
        ld_dn = [sem(f"ld_dn{i}") for i in range(2)]
        ld_cond = sem("ld_cond")
        ld_gb = sem("ld_gb")
        ld_b = sem("ld_b")
        ld_w = sem("ld_w")
        ld_qk = sem("ld_qk")
        ld_ab = sem("ld_ab")
        s_ones = sem("s_ones")
        s_ident = sem("s_ident")
        s_zero = sem("s_zero")
        s_gmask = sem("s_gmask")
        s_cTp = sem("s_cTp")
        s_cT = sem("s_cT")
        s_prod0 = sem("s_prod0")
        s_prod0h = sem("s_prod0h")
        s_prod0s = sem("s_prod0s")
        s_wcp = sem("s_wcp")
        s_wcT = sem("s_wcT")
        s_wconv = sem("s_wconv")
        s_B0p = sem("s_B0p")
        s_B0 = sem("s_B0")
        s_exTp = sem("s_exTp")
        s_exTh = sem("s_exTh")
        s_exT = sem("s_exT")
        s_fc2h = sem("s_fc2h")
        s_fc2 = sem("s_fc2")
        s_E2p = sem("s_E2p")
        s_E2h = sem("s_E2h")
        s_E2 = sem("s_E2")
        s_c1p = sem("s_c1p")
        s_c1 = sem("s_c1")
        s_c2p = sem("s_c2p")
        s_c2 = sem("s_c2")
        s_lgp = sem("s_lgp")
        s_att = sem("s_att")
        s_aexp = sem("s_aexp")
        s_aTp = sem("s_aTp")
        s_aT = sem("s_aT")
        s_prod1 = sem("s_prod1")
        s_prod1h = sem("s_prod1h")
        s_prod1s = sem("s_prod1s")
        s_AGp = sem("s_AGp")
        s_agg = sem("s_agg")
        s_BD = sem("s_BD")
        s_B1p = sem("s_B1p")
        s_B1 = sem("s_B1")
        s_uph = sem("s_uph")
        s_up = sem("s_up")
        s_fch = sem("s_fch")
        s_fc = sem("s_fc")
        s_dnh = sem("s_dnh")
        s_dn = sem("s_dn")
        s_wgt = sem("s_wgt")
        s_wgh = sem("s_wgh")
        s_wg = sem("s_wg")
        xs_v = sem("xs_v")
        xs_a = sem("xs_a")
        s_conv = sem("s_conv")
        s_tf = sem("s_tf")
        s_Hh = sem("s_Hh")
        s_H = sem("s_H")
        s_gatez = sem("s_gatez")
        s_gateh = sem("s_gateh")
        s_gate = sem("s_gate")
        s_logit = sem("s_logit")
        s_gT = sem("s_gT")
        s_gTs = sem("s_gTs")
        s_gp = sem("s_gp")
        s_top = sem("s_top")
        s_sum = sem("s_sum")
        s_sumh = sem("s_sumh")
        s_suml = sem("s_suml")
        s_diag = sem("s_diag")
        s_diagl = sem("s_diagl")
        s_sbp = sem("s_sbp")
        s_sb = sem("s_sb")
        s_latp = sem("s_latp")
        s_lats = sem("s_lats")
        s_lath = sem("s_lath")
        s_lat = sem("s_lat")
        s_upp = sem("s_upp")
        s_relu = sem("s_relu")
        s_sq = sem("s_sq")
        s_Rh = sem("s_Rh")
        s_R = sem("s_R")
        s_down = sem("s_down")
        s_ffn = sem("s_ffn")
        s_bn = sem("s_bn")
        s_mv = sem("s_mv")
        s_ve = sem("s_ve")
        s_rstd = sem("s_rstd")
        s_cen = sem("s_cen")
        s_x1 = sem("s_x1")
        s_xb = sem("s_xb")
        s_yp = sem("s_yp")
        s_yb = sem("s_yb")
        s_Yh = sem("s_Yh")
        s_Y = sem("s_Y")
        s_x1b = sem("s_x1b")
        s_qkp = sem("s_qkp")
        s_q = sem("s_q")
        s_pr = sem("s_pr")
        s_sc = sem("s_sc")
        s_mx = sem("s_mx")
        s_nmx = sem("s_nmx")
        s_e = sem("s_e")
        s_rc = sem("s_rc")
        s_hw = sem("s_hw")
        s_hwp = sem("s_hwp")
        s_hwh = sem("s_hwh")
        s_hwT = sem("s_hwT")
        s_res = sem("s_res")
        s_fin = sem("s_fin")
        s_out = sem("s_out")

        block = ctx.enter_context(nc.Block())

        G0 = PH
        NG = 2 * PH + 2

        def wg_src(g):
            if g < PH:
                return qk_raw[:, g]
            if g < 2 * PH:
                return w_raw[:, g - PH]
            return a_raw.rearrange("p c (a q) -> p c a q", a=2) if g == 2 * PH else b_raw

        def wg_dst(g, hi):
            if g < PH:
                return (qkT_hi if hi else qkT_lo)[:, g, :, 0:QW]
            if g < 2 * PH:
                return (wT_hi if hi else wT_lo)[:, g - PH]
            if g == 2 * PH:
                return (qkT_hi if hi else qkT_lo)[:, :, :, QW:QKW]
            return (bT_hi if hi else bT_lo)[:]

        def wg_turned(g):
            flat = fc_raw[:].rearrange("p a b -> p (a b)") if g < G0 else qk_raw[:].rearrange("p c a q -> p (c a q)")
            n = (fc_raw.shape[1] * fc_raw.shape[2] if g < G0 else PH * L) // L
            v = flat[:, g % n * L:(g % n + 1) * L]
            if g < PH:
                return v.rearrange("p (a q) -> p a q", a=2)
            return v.rearrange("p (c a q) -> p c a q", c=PH, a=2) if g == 2 * PH else v

        def groups_after(h, c):
            if h == 0:
                return [c - PH] if c >= PH else []
            return {4: [G0], 5: [G0 + 1, G0 + 2], 6: [G0 + 3, G0 + 4], 7: [G0 + 5]}.get(c, [])

        def conv_bank(T):
            return ((U[0], U[1], D[2], D[3]), (U[0], U[1], M[0], M[1]))[T // TPH][T % TPH]

        def mix_bank(T):
            return (M[T] if T < 2 else D[T % TPH]).rearrange("p (c t) -> p c t", c=PH)

        def bcast_mid(ap, n):
            return ap.unsqueeze(1).broadcast_to([ap.shape[0], n, *ap.shape[1:]])

        def down_done(eng, i):
            h, c = divmod(i, IC)
            if c == IC - 1:
                eng.wait_ge(s_ffn, TPH * (h + 1))
            else:
                eng.wait_ge(s_down, h * (IC - 1) + c + 1)

        XPARTS = [(0, 1), (1, 2), (2, TPH), (TPH, TILES)]

        def phase_copies(eng, t0, t1):
            for s in range(SPT):
                for j in range(PH):
                    if (PH * s + j < 10) == (eng is nc.vector):
                        last = phase_copy(eng, s, j, t0, t1)
            return last

        def phase_copy(eng, s, j, t0, t1):
            src = X[C * s:C * (s + 1), t0:t1, :].rearrange("p t (m j) -> p t m j", j=PH)[:, :, :, j]
            a, b = t0 % TPH, (t1 - 1) % TPH + 1
            dst = XS[C * j:C * (j + 1), a * SPT:b * SPT, 1:1 + P]\
                .rearrange("p (t s) m -> p t s m", s=SPT)[:, :, s]
            if eng is nc.vector:
                return nc.vector.tensor_copy(dst, src)
            return nc.scalar.activation(dst, src, ACT.Copy)

        @block.sync
        def _(sp):
            def load_x(i):
                t0, t1 = XPARTS[i]
                sp.dma_start(X[:, t0:t1, :], xt_dram[:, t0:t1, :]).then_inc(ld_x[i], 16)

            load_x(0)
            sp.dma_start(c_nat[:], cond_128).then_inc(ld_c, 16)
            load_x(1)
            load_x(2)
            sp.dma_start(fsb[:], fside_S_0.partition_broadcast(P)).then_inc(ld_fs, 16)
            sp.dma_start(exraw[:], L0_ffn_expert_w.rearrange("(c p) m -> p c m", p=P)).then_inc(ld_ex, 16)
            for dst, src in ((W0, L1_cond_W0), (W1, L1_cond_W1), (W2, L1_cond_W2), (bk, L1_cond_bias_k)):
                sp.dma_start(dst[:], src).then_inc(ld_cond, 16)
            for dst, src in ((b0, L1_cond_b0), (b1, L1_cond_b1)):
                sp.dma_start(dst[:], src.rearrange("(p a) -> p a", a=1)).then_inc(ld_cond, 16)
            sp.dma_start(b2[:], L1_cond_b2.partition_broadcast(N)).then_inc(ld_cond, 16)
            sp.dma_start(wk[:], L1_cond_weight.rearrange("k o i a -> k o (i a)")).then_inc(ld_cond, 16)
            sp.dma_start(fc2[:], L0_ffn_fc2_w.rearrange("(c p) l -> p c l", p=P)).then_inc(ld_fc2, 16)
            sp.dma_start(gate[:], L0_ffn_gate_w.rearrange("(m p) e -> m p e", p=PH)).then_inc(ld_gate, 16)
            upv = L0_ffn_up_w.rearrange("(m p) i -> m p i", p=PH)
            sp.dma_start(up_raw[:, :, 0:INT // 2], upv[:, :, 0:INT // 2]).then_inc(ld_up[0], 16)
            sp.dma_start(fc_raw[:], L0_ffn_fc1_w.rearrange("(m p) i -> m p i", p=PH)).then_inc(ld_fc, 16)
            sp.dma_start(up_raw[:, :, INT // 2:INT], upv[:, :, INT // 2:INT]).then_inc(ld_up[1], 16)
            dnv = L0_ffn_down_w.rearrange("(c p) l -> p c l", p=P)
            for i in range(2):
                cs = slice(i * IC // 2, (i + 1) * IC // 2)
                sp.dma_start(dn_raw[:, cs, :], dnv[:, cs, :]).then_inc(ld_dn[i], 16)
            load_x(3)
            sp.dma_start(gamma[:], L0_ffn_ln_gamma.partition_broadcast(P)).then_inc(ld_gb, 16)
            sp.dma_start(rowb[:], L0_ffn_ln_beta.partition_broadcast(P)).then_inc(ld_gb, 16)

            def load_blocks(dst, w, sem_):
                wv = w.rearrange("(j c) (p a r) -> a p c j r", c=C, p=PH, r=C)
                for a in range(PH):
                    for p in range(PH):
                        sp.dma_start(dst[C * a:C * (a + 1), p].rearrange("c (j r) -> c j r", r=C), wv[a, p])\
                            .then_inc(sem_, 16)

            for i, w in enumerate((L1_ffn_Wq, L1_ffn_Wk)):
                load_blocks(qk_raw[:, :, i], w, ld_qk)
            sp.wait_ge(s_conv, TILES)
            load_blocks(w_raw, L1_ffn_W, ld_w)
            sp.wait_ge(s_H, TILES)
            load_blocks(a_raw, L1_ffn_A.rearrange("e r l -> (e r) l"), ld_ab)
            epb = C // R
            for a in range(PH):
                for e in range(epb):
                    bv = L1_ffn_Bm[a * epb + e].rearrange("(j c) r -> c j r", c=C)
                    sp.dma_start(b_raw[C * a:C * (a + 1)].rearrange("c (j e r) -> c j e r", e=epb, r=R)[:, :, e], bv)\
                        .then_inc(ld_ab, 16)
            sp.wait_ge(s_xb, TILES)
            sp.dma_start(rowb[:], L1_ffn_b.partition_broadcast(P)).then_inc(ld_b, 16)
            for T in range(TILES):
                sp.wait_ge(s_fin, T + 1)
                sp.dma_start(out_dram[:, T, :], X[:, T, :]).then_inc(s_out, 16)
            sp.wait_ge(s_out, 16 * TILES)

        @block.gpsimd
        def _(pool):
            nc.gpsimd.memset(ident[:], 0.0).then_inc(s_ident, 1)
            nc.gpsimd.memset(wc_pad[:], 0.0).then_inc(s_zero, 1)
            pool.wait_ge(s_ident, 1)
            nc.gpsimd.affine_select(out=ident[:], in_=ident[:], compare_op=ALU.not_equal, fill=1.0, base=0,
                                    pattern=[[-1, P]], channel_multiplier=1).then_inc(s_ident, 1)
            nc.gpsimd.memset(gmask[:], 1.0).then_inc(s_gmask, 1)
            pool.wait_ge(s_gmask, 1)
            nc.gpsimd.affine_select(out=gmask[:], in_=gmask[:], compare_op=ALU.is_ge, fill=0.0, base=0,
                                    pattern=[[-CG, G]], channel_multiplier=1).then_inc(s_gmask, 1)
            pool.wait_ge(s_gmask, 2)
            nc.gpsimd.affine_select(out=gmask[:], in_=gmask[:], compare_op=ALU.is_ge, fill=0.0, base=CG - 1,
                                    pattern=[[CG, G]], channel_multiplier=-1).then_inc(s_gmask, 1)
            nc.gpsimd.memset(XS[:, :, 0:1], 0.0)
            nc.gpsimd.memset(XS[:, :, XW - 1:XW], 0.0).then_inc(s_zero, 1)
            pool.wait_ge(s_cT, 1)
            nc.gpsimd.tensor_tensor(prod0[:], bcast_mid(cwT[:], N), cT[:].unsqueeze(2).broadcast_to([CD, N, C]),
                                    ALU.mult).then_inc(s_prod0, 1)
            nc.gpsimd.memset(nhalf[:], -0.5)
            nc.gpsimd.memset(gate_hl[:].bitcast(mybir.dt.uint32), 0).then_inc(s_gatez, 1)
            nc.gpsimd.memset(BD[:], 0.0).then_inc(s_zero, 1)
            pool.wait_ge(s_fc2h, 1)
            nc.gpsimd.tensor_tensor(fc2_lo, fc2[:], fc2_hi.bitcast(F32), ALU.subtract).then_inc(s_fc2, 1)
            pool.wait_ge(s_fch, 1)
            nc.gpsimd.tensor_tensor(fc_lo[:], fc_raw[:], fc_hi[:].bitcast(F32), ALU.subtract).then_inc(s_fc, 1)

            def split_dn(c):
                pool.wait_ge(s_dnh, c + 1)
                nc.gpsimd.tensor_tensor(dn_lo[:, c, :], dn_raw[:, c, :], dn_hi[:, c, :].bitcast(F32),
                                        ALU.subtract).then_inc(s_dn, 1)

            split_dn(0)
            pool.wait_ge(s_zero, 3)
            pool.wait_ge(s_agg, 2)
            pool.wait_ge(s_dn, 1)
            for s in range(SPT):
                if s:
                    pool.wait_ge(s_BD, s)
                nc.gpsimd.tensor_copy(BD[C * s:C * (s + 1), :, C * s:C * (s + 1)],
                                      agg.rearrange("p o (t s) -> p s t o", s=SPT)[:, s]).then_inc(s_BD, 1)
            pool.wait_ge(s_BD, SPT)

            def add_beta(T):
                if T == 0:
                    pool.wait_ge(ld_gb, 32)
                if T % TPH == 0:
                    pool.wait_ge(xs_v, 3 + T // TPH)
                    pool.wait_ge(xs_a, 3 + T // TPH)
                nc.gpsimd.tensor_tensor(X[:, T, :], X[:, T, :], rowb[:], ALU.add).then_inc(s_xb, 1)

            def norm_scale(T):
                t = T % TPH
                pool.wait_ge(s_mv, T + 1)
                if T >= TPH:
                    pool.wait_ge(s_x1, T - TPH + 1)
                nc.gpsimd.tensor_scalar(ve[:, t:t + 1], mv[:, t, 1:2], EPS, 1.0, ALU.add, ALU.mult)\
                    .then_inc(s_ve, 1)
                pool.wait_ge(s_ve, T + 1)
                nc.gpsimd.tensor_tensor(rstd[:, t:t + 1], ve[:, t:t + 1], nhalf[:], ALU.pow).then_inc(s_rstd, 1)

            def add_bias(h):
                for t in range(TPH):
                    T = h * TPH + t
                    pool.wait_ge(s_yp, T + 1)
                    nc.gpsimd.tensor_tensor(X[:, T, :], X[:, T, :], rowb[:], ALU.add).then_inc(s_x1b, 1)

            def group_split(g):
                pool.wait_ge(s_wgh, g + 1)
                nc.gpsimd.tensor_tensor(wg_dst(g, False), wg_turned(g), wg_dst(g, True).bitcast(F32), ALU.subtract)\
                    .then_inc(s_wg, 1)

            for c in range(1, IC):
                split_dn(c)
                if 3 <= c < 3 + TPH:
                    add_beta(c - 3)
                for g in groups_after(0, c):
                    group_split(g)
            for T in range(TPH):
                norm_scale(T)
            for T in range(TPH, TILES):
                add_beta(T)
            for g in range(G0, NG):
                group_split(g)
            for T in range(TPH, TILES):
                norm_scale(T)
            pool.wait_ge(ld_b, 16)
            add_bias(0)
            add_bias(1)

        @block.scalar
        def _(act):
            act.dma_start(wc_nat[:], L0_cond_weight).then_inc(ld_wc, 16)
            act.dma_start(cw_nat[:], L0_cond_c_weight).then_inc(ld_c, 16)
            act.wait_ge(s_ones, 1)
            nc.scalar.activation(ones_r[:], ones[:], ACT.Copy).then_inc(s_ones, 1)

            def shift_copies(i):
                act.wait_ge(ld_x[i], 16)
                phase_copies(nc.scalar, *XPARTS[i]).then_inc(xs_a, 1)

            def split_up(c):
                act.wait_ge(ld_up[c // (IC // 2)], 16)
                nc.scalar.activation(up_hi[:, c], up_raw[:, :, c * P:(c + 1) * P], ACT.Copy).then_inc(s_uph, 1)

            def split_dn(c):
                act.wait_ge(ld_dn[c // (IC // 2)], 16)
                nc.scalar.activation(dn_hi[:, c, :], dn_raw[:, c, :], ACT.Copy).then_inc(s_dnh, 1)

            def split_H(T):
                t = T % TPH
                act.wait_ge(s_tf, T + 1)
                nc.scalar.activation(H_hi[:, :, t * P:(t + 1) * P], tf[:, T % 2], ACT.Copy).then_inc(s_Hh, 1)

            def up_relu(i):
                act.wait_ge(s_upp, i + 1)
                if i:
                    act.wait_ge(s_sq, i)
                nc.scalar.activation(relu[:], U[i % 2], ACT.Relu).then_inc(s_relu, 1)

            def up_split(i):
                act.wait_ge(s_sq, i + 1)
                if i >= NR:
                    down_done(act, i - NR)
                nc.scalar.activation(R_hi[i % NR], U[i % 2], ACT.Copy).then_inc(s_Rh, 1)

            def scale_rows(h):
                act.wait_ge(s_sbp, h + 1)
                nc.scalar.activation(sbc[:], M[0], ACT.Copy).then_inc(s_sb, 1)

            def diag_low(h):
                act.wait_ge(s_suml, h + 1)
                for t in range(TPH):
                    last = nc.scalar.activation(diag_lo[:, t * P:(t + 1) * P], ident[:], ACT.Copy,
                                                scale=ssum_lo[:, t:t + 1].bitcast(F32))
                last.then_inc(s_diagl, 1)

            def gate_copy(h):
                act.wait_ge(s_gT, h + 1)
                if h:
                    act.wait_ge(s_lats, LC)
                nc.scalar.activation(sbc[0:2 * NE, :], M[0][0:2 * NE, :], ACT.Copy).then_inc(s_gTs, 1)

            def lat_split(n):
                act.wait_ge(s_lats, n + 1)
                if n == 0:
                    act.wait_ge(s_BD, SPT)
                nc.scalar.activation(lat_hi[:, n % LC], M[(n + 1) % LC], ACT.Copy).then_inc(s_lath, 1)

            def group_split(g):
                act.wait_ge(s_wgt, g + 1)
                nc.scalar.activation(wg_dst(g, True), wg_turned(g), ACT.Copy).then_inc(s_wgh, 1)

            for i in range(3):
                shift_copies(i)
            act.wait_ge(s_prod0, 1)
            nc.scalar.activation(prod0_hi, prod0[:].rearrange("d n o -> d (n o)"), ACT.Copy).then_inc(s_prod0h, 1)
            act.wait_ge(s_exTp, 1)
            nc.scalar.activation(exT_hi.rearrange("p c m -> p (c m)"), M[1], ACT.Copy).then_inc(s_exTh, 1)
            act.wait_ge(ld_fc2, 16)
            nc.scalar.activation(fc2_hi, fc2[:], ACT.Copy).then_inc(s_fc2h, 1)
            act.wait_ge(ld_cond, 16 * 8)
            act.wait_ge(s_c1p, 1)
            nc.scalar.activation(h1[:], M[0][:, 0:N], ACT.Gelu, bias=b0[:, 0:1]).then_inc(s_c1, 1)
            split_H(0)
            split_up(0)
            act.wait_ge(s_c2p, 1)
            nc.scalar.activation(h2[:], M[0][:, 0:N], ACT.Gelu, bias=b1[:, 0:1]).then_inc(s_c2, 1)
            split_H(1)
            split_up(1)
            split_H(2)
            act.wait_ge(s_att, 3)
            nc.scalar.activation(att[:, 2, :], att[:, 1, :], ACT.Exp, accum_out=att[:, 3, 0:1]).then_inc(s_aexp, 1)
            split_H(3)
            for i in range(LC):
                act.wait_ge(s_E2p, i + 1)
                nc.scalar.activation(ex_hi[:, i, :], D[i], ACT.Copy).then_inc(s_E2h, 1)
            act.wait_ge(s_aTp, 1)
            nc.scalar.activation(attT[:], M[0][0:KE, 0:N], ACT.Copy).then_inc(s_aT, 1)
            act.wait_ge(ld_gate, 16)
            act.wait_ge(s_gatez, 1)
            nc.scalar.activation(gate_hl[:, :, 0:NE], gate[:], ACT.Copy).then_inc(s_gateh, 1)
            act.wait_ge(ld_fc, 16)
            nc.scalar.activation(fc_hi[:], fc_raw[:], ACT.Copy).then_inc(s_fch, 1)
            split_up(2)
            split_up(3)
            split_up(4)
            act.wait_ge(s_prod1, 1)
            nc.scalar.activation(prod1_hi, prod1[:].rearrange("k n o -> k (n o)"), ACT.Copy).then_inc(s_prod1h, 1)

            def make_B1():
                for i in range(2):
                    act.wait_ge(s_B1p, i + 1)
                    nc.scalar.activation(B1[:, i * BANK:(i + 1) * BANK], D[2 + i], ACT.Copy).then_inc(s_B1, 1)

            for h in range(HALVES):
                i0 = h * IC
                if h:
                    for t in range(TPH):
                        split_H(TPH + t)
                up_relu(i0)
                if h == 0:
                    gate_copy(h)
                    up_split(i0)
                else:
                    up_split(i0)
                    gate_copy(h)
                up_relu(i0 + 1)
                if h == 0:
                    split_dn(0)
                diag_low(h)
                if h == 0:
                    make_B1()
                scale_rows(h)
                up_split(i0 + 1)
                if h == 0:
                    split_up(5)
                up_relu(i0 + 2)
                up_split(i0 + 2)
                for n in range(LC):
                    if h == 0:
                        split_dn(1 + n)
                        split_up(6 + n)
                    lat_split(h * LC + n)
                for c in range(3, IC):
                    if h == 0:
                        split_dn(c)
                    up_relu(i0 + c)
                    up_split(i0 + c)
                    if h == 0 and c == 3:
                        act.wait_ge(s_conv, TPH)
                        shift_copies(3)
                    for g in groups_after(h, c):
                        group_split(g)

            def y_split(T):
                t = T % TPH
                act.wait_ge(s_yb, T + 1)
                nc.scalar.activation(H_hi[:, :, t * P:(t + 1) * P],
                                     mix_bank(T), ACT.Copy).then_inc(s_Yh, 1)

            def q_copy(T):
                act.wait_ge(s_qkp, T + 1)
                if T:
                    act.wait_ge(s_pr, T)
                nc.scalar.activation(qs[:], QK[T % 2][0][:, 0:QW], ACT.Copy).then_inc(s_q, 1)

            def exp_scores(T):
                act.wait_ge(s_nmx, T + 1)
                nc.scalar.activation(sm[:, T % 2, 2, :], sm[:, T % 2, 0, :], ACT.Exp, scale=SCALE,
                                     bias=sm[:, T % 2, 1, 1:2], accum_out=sm[:, T % 2, 3, 0:1]).then_inc(s_e, 1)

            def hw_split(T):
                act.wait_ge(s_hwp, T + 1)
                if T >= 2:
                    act.wait_ge(s_res, T - 1)
                nc.scalar.activation(hwT_hi[:, T % 2], QK[T % 2][0][:, 0:P], ACT.Copy).then_inc(s_hwh, 1)

            y_split(0)
            y_split(1)
            q_copy(0)
            exp_scores(0)
            q_copy(1)
            hw_split(0)
            y_split(2)
            exp_scores(1)
            y_split(3)
            for T in range(1, TILES - 3):
                q_copy(T + 1)
                hw_split(T)
                exp_scores(T + 1)
                y_split(T + 3)
            _, b, c, d = range(TILES - 4, TILES)
            hw_split(b)
            q_copy(c)
            exp_scores(c)
            q_copy(d)
            exp_scores(d)
            hw_split(c)
            hw_split(d)

        @block.vector
        def _(dve):
            def shift_copies(i):
                dve.wait_ge(ld_x[i], 16)
                phase_copies(nc.vector, *XPARTS[i]).then_inc(xs_v, 1)

            def split_up(c):
                dve.wait_ge(s_uph, c + 1)
                nc.vector.tensor_tensor(up_lo[:, c], up_raw[:, :, c * P:(c + 1) * P], up_hi[:, c].bitcast(F32),
                                        ALU.subtract).then_inc(s_up, 1)

            def add_ctx(T):
                dve.wait_ge(s_conv, T + 1)
                if T == 0:
                    dve.wait_ge(s_B0, 2)
                if T >= 2:
                    dve.wait_ge(s_H, T - 1)
                nc.vector.tensor_tensor(
                    tf[:, T % 2].rearrange("m p (n o) -> m n p o", o=C),
                    conv_bank(T).rearrange("m (n p o) -> m n p o", n=SPT, p=PH),
                    B0[:, T * P:(T + 1) * P].rearrange("m (n o) -> m n o", o=C).unsqueeze(2)
                    .broadcast_to([P, SPT, PH, C]), ALU.add).then_inc(s_tf, 1)

            def split_H(T):
                t = T % TPH
                dve.wait_ge(s_Hh, T + 1)
                hs = slice(t * P, (t + 1) * P)
                nc.vector.tensor_tensor(H_lo[:, :, hs], tf[:, T % 2], H_hi[:, :, hs].bitcast(F32),
                                        ALU.subtract).then_inc(s_H, 1)

            def gate_sum(h):
                dve.wait_ge(s_gp, h + 1)
                parts = M[1][:, 0:TPH * 2 * NE].rearrange("p (t v e) -> p t e v", t=TPH, v=2)
                nc.vector.reduce_sum(logit[:], parts, AX_X).then_inc(s_logit, 1)
                dve.wait_ge(s_logit, h + 1)
                for t in range(TPH):
                    last = nc.vector.max(top[:, t], logit[:, t])
                last.then_inc(s_top, 1)
                dve.wait_ge(s_top, h + 1)
                nc.vector.tensor_tensor(ssum[:].unsqueeze(2), top[:, :, 0:1], top[:, :, 1:2], ALU.add)\
                    .then_inc(s_sum, 1)
                dve.wait_ge(s_sum, h + 1)
                nc.vector.tensor_copy(ssum_hi[:], ssum[:]).then_inc(s_sumh, 1)
                dve.wait_ge(s_sumh, h + 1)
                nc.vector.tensor_tensor(ssum_lo[:], ssum[:], ssum_hi[:].bitcast(F32), ALU.subtract).then_inc(s_suml, 1)
                for t in range(TPH):
                    last = nc.vector.tensor_scalar(diag_hi[:, t * P:(t + 1) * P], ident[:],
                                                   ssum_hi[:, t:t + 1].bitcast(F32), None, ALU.mult)
                last.then_inc(s_diag, 1)

            def up_square(i):
                dve.wait_ge(s_relu, i + 1)
                nc.vector.tensor_tensor(U[i % 2], U[i % 2], relu[:], ALU.mult).then_inc(s_sq, 1)

            def up_split(i):
                dve.wait_ge(s_Rh, i + 1)
                nc.vector.tensor_tensor(R_lo[i % NR], U[i % 2], R_hi[i % NR].bitcast(F32),
                                        ALU.subtract).then_inc(s_R, 1)

            def lat_scale(n):
                dve.wait_ge(s_latp, n + 1)
                dve.wait_ge(s_sb, n // LC + 1)
                b = M[(n + 1) % LC]
                nc.vector.tensor_tensor(b, b, sbc[:], ALU.mult).then_inc(s_lats, 1)

            def lat_split(n):
                dve.wait_ge(s_lath, n + 1)
                nc.vector.tensor_tensor(lat_lo[:, n % LC], M[(n + 1) % LC], lat_hi[:, n % LC].bitcast(F32),
                                        ALU.subtract).then_inc(s_lat, 1)

            def turn_group(g):
                if g == 0:
                    dve.wait_ge(ld_qk, 16 * 2 * PH * PH)
                    dve.wait_ge(s_fc, 1)
                    dve.wait_ge(s_dn, IC // 2)
                elif g == G0:
                    dve.wait_ge(ld_w, 16 * PH * PH)
                    dve.wait_ge(s_dn, IC)
                elif g == 2 * PH:
                    dve.wait_ge(ld_ab, 16 * (PH * PH + E))
                if 2 <= g < G0:
                    dve.wait_ge(s_wg, g - 1)
                elif g >= 2 * G0:
                    dve.wait_ge(s_wg, g - G0 + 1)
                nc.vector.transpose(wg_turned(g), wg_src(g)).then_inc(s_wgt, 1)

            def norm_stats(T):
                dve.wait_ge(s_ffn, T + 1)
                nc.vector.bn_stats(st6[:, T % 2], D[T % TPH]).then_inc(s_bn, 1)
                dve.wait_ge(s_bn, T + 1)
                if T >= TPH:
                    dve.wait_ge(s_ve, T - TPH + 1)
                nc.vector.bn_aggr(mv[:, T % TPH], st6[:, T % 2]).then_inc(s_mv, 1)
                dve.wait_ge(s_mv, T + 1)
                if T == 0:
                    dve.wait_ge(ld_gb, 32)
                nc.vector.scalar_tensor_tensor(D[T % TPH], D[T % TPH], mv[:, T % TPH, 0:1], gamma[:],
                                               ALU.subtract, ALU.mult).then_inc(s_cen, 1)

            def norm_apply(T):
                dve.wait_ge(s_rstd, T + 1)
                dve.wait_ge(s_cen, T + 1)
                dve.wait_ge(s_xb, T + 1)
                nc.vector.scalar_tensor_tensor(X[:, T, :], D[T % TPH], rstd[:, T % TPH:T % TPH + 1], X[:, T, :],
                                               ALU.mult, ALU.add).then_inc(s_x1, 1)

            nc.vector.memset(ones[:], 1.0).then_inc(s_ones, 1)
            dve.wait_ge(ld_wc, 16)
            dve.wait_ge(s_zero, 1)
            dve.wait_ge(s_gmask, 3)
            nc.vector.tensor_tensor(
                wc_pad[:, PH - 1:PH - 1 + KT, :].rearrange("p k (g i) -> p k g i", g=G),
                wc_nat[:].rearrange("p i k -> p k i").unsqueeze(2).broadcast_to([C, KT, G, CG]),
                gmask[:].unsqueeze(1).unsqueeze(3).broadcast_to([C, KT, G, CG]), ALU.mult).then_inc(s_wcp, 1)
            shift_copies(0)
            dve.wait_ge(s_wcT, 1)
            nc.vector.tensor_copy(wconv[:].rearrange("p a q -> p (a q)"), M[1][:, 0:NWIN * P]).then_inc(s_wconv, 1)
            dve.wait_ge(s_cTp, 1)
            nc.vector.tensor_copy(cT[:], M[0][:, 0:N])
            nc.vector.tensor_copy(cwT[:], M[0][:, N:N + C]).then_inc(s_cT, 1)
            shift_copies(1)
            shift_copies(2)
            dve.wait_ge(s_prod0h, 1)
            nc.vector.tensor_tensor(prod0_lo, prod0[:].rearrange("d n o -> d (n o)"), prod0_hi.bitcast(F32),
                                    ALU.subtract).then_inc(s_prod0s, 1)
            dve.wait_ge(s_exTh, 1)
            nc.vector.tensor_tensor(exT_lo.rearrange("p c m -> p (c m)"), M[1],
                                    exT_hi.rearrange("p c m -> p (c m)").bitcast(F32), ALU.subtract).then_inc(s_exT, 1)
            dve.wait_ge(ld_fs, 16)
            for i in range(2):
                dve.wait_ge(s_B0p, i + 1)
                nc.vector.tensor_tensor(B0[:, i * BANK:(i + 1) * BANK].rearrange("p (n o) -> p n o", o=C),
                                        D[i].rearrange("p (n o) -> p n o", o=C), bcast_mid(fsb[:], BANK // C),
                                        ALU.add).then_inc(s_B0, 1)
            add_ctx(0)
            add_ctx(1)
            split_H(0)
            split_up(0)
            add_ctx(2)
            split_H(1)
            split_up(1)
            dve.wait_ge(s_lgp, 1)
            nc.vector.tensor_tensor(att[:, 0, :], M[0][0:N, 0:KE], b2[:], ALU.add).then_inc(s_att, 1)
            dve.wait_ge(s_att, 1)
            nc.vector.reduce_max(att[:, 3, 1:2], att[:, 0, :], AX_X).then_inc(s_att, 1)
            dve.wait_ge(s_att, 2)
            nc.vector.tensor_scalar(att[:, 1, :], att[:, 0, :], att[:, 3, 1:2], None, ALU.subtract).then_inc(s_att, 1)
            add_ctx(3)
            split_H(2)
            dve.wait_ge(s_aexp, 1)
            nc.vector.reciprocal(att[:, 3, 2:3], att[:, 3, 0:1]).then_inc(s_att, 1)
            dve.wait_ge(s_att, 4)
            nc.vector.tensor_scalar(att[:, 0, :], att[:, 2, :], att[:, 3, 2:3], None, ALU.mult).then_inc(s_att, 1)
            split_H(3)
            dve.wait_ge(s_E2p, LC)
            for i in range(LC):
                dve.wait_ge(s_E2h, i + 1)
                nc.vector.tensor_tensor(ex_lo[:, i, :], D[i], ex_hi[:, i, :].bitcast(F32),
                                        ALU.subtract).then_inc(s_E2, 1)
            dve.wait_ge(s_gateh, 1)
            nc.vector.tensor_tensor(gate_hl[:, :, NE:2 * NE], gate[:], gate_hl[:, :, 0:NE].bitcast(F32),
                                    ALU.subtract).then_inc(s_gate, 1)
            dve.wait_ge(s_aT, 1)
            nc.vector.tensor_tensor(prod1[:], bcast_mid(bk[:], N), attT[:].unsqueeze(2).broadcast_to([KE, N, C]),
                                    ALU.mult).then_inc(s_prod1, 1)
            split_up(2)
            split_up(3)
            split_up(4)

            def split_prod1():
                dve.wait_ge(s_prod1h, 1)
                nc.vector.tensor_tensor(prod1_lo, prod1[:].rearrange("k n o -> k (n o)"), prod1_hi.bitcast(F32),
                                        ALU.subtract).then_inc(s_prod1s, 1)

            def turn_agg():
                dve.wait_ge(s_AGp, 1)
                for b in range(2):
                    nc.vector.transpose(agg[:, b * (C // 2):(b + 1) * (C // 2), :].rearrange("i o n -> i (o n)"),
                                        D[b][0:C, :]).then_inc(s_agg, 1)

            for h in range(HALVES):
                i0 = h * IC
                if h:
                    norm_stats(0)
                    norm_stats(1)
                    norm_apply(0)
                    norm_stats(2)
                    norm_apply(1)
                    add_ctx(TPH)
                    norm_apply(2)
                    split_H(TPH)
                    for T in range(TPH + 1, TILES):
                        add_ctx(T)
                        split_H(T)
                    norm_stats(3)
                    norm_apply(3)
                up_square(i0)
                if h == 0:
                    split_prod1()
                up_split(i0)
                gate_sum(h)
                if h == 0:
                    turn_agg()
                up_square(i0 + 1)
                up_split(i0 + 1)
                if h == 0:
                    split_up(5)
                up_square(i0 + 2)
                up_split(i0 + 2)
                for n in range(LC):
                    if h == 0:
                        split_up(6 + n)
                    lat_scale(h * LC + n)
                    lat_split(h * LC + n)
                for c in range(3, IC):
                    up_square(i0 + c)
                    up_split(i0 + c)
                    if h == 0 and c == 3:
                        shift_copies(3)
                    for g in groups_after(h, c):
                        turn_group(g)

            def y_bias(T):
                dve.wait_ge(s_yp, T + 1)
                b = mix_bank(T)
                nc.vector.tensor_tensor(b, b, bcast_mid(B1[:, T * P:(T + 1) * P], PH), ALU.add).then_inc(s_yb, 1)

            def y_split(T):
                hs = slice(T % TPH * P, (T % TPH + 1) * P)
                dve.wait_ge(s_Yh, T + 1)
                nc.vector.tensor_tensor(H_lo[:, :, hs], mix_bank(T), H_hi[:, :, hs].bitcast(F32),
                                        ALU.subtract).then_inc(s_Y, 1)

            def scores(T):
                s = sm[:, T % 2]
                dve.wait_ge(s_q, T + 1)
                nc.vector.tensor_tensor(pr[:], QK[T % 2][1][:, 0:QW], qs[:], ALU.mult).then_inc(s_pr, 1)
                dve.wait_ge(s_pr, T + 1)
                nc.vector.reduce_sum(s[:, 0, :], pr[:].rearrange("p (e d) -> p e d", e=E), AX_X).then_inc(s_sc, 1)
                dve.wait_ge(s_sc, T + 1)
                nc.vector.reduce_max(s[:, 1, 0:1], s[:, 0, :], AX_X).then_inc(s_mx, 1)
                dve.wait_ge(s_mx, T + 1)
                nc.vector.tensor_scalar(s[:, 1, 1:2], s[:, 1, 0:1], -SCALE, None, ALU.mult).then_inc(s_nmx, 1)

            def weigh(T):
                s = sm[:, T % 2]
                dve.wait_ge(s_e, T + 1)
                nc.vector.reciprocal(s[:, 3, 1:2], s[:, 3, 0:1]).then_inc(s_rc, 1)
                dve.wait_ge(s_rc, T + 1)
                if T:
                    dve.wait_ge(s_hwp, T)
                for a in range(2):
                    last = nc.vector.scalar_tensor_tensor(
                        hw[:, a * HH:(a + 1) * HH].rearrange("p (e r) -> p e r", e=EH),
                        QK[T % 2][a][:, QW:QKW].rearrange("p (e r) -> p e r", e=EH), s[:, 3, 1:2],
                        s[:, 2, a * EH:(a + 1) * EH].unsqueeze(2).broadcast_to([P, EH, R]), ALU.mult, ALU.mult)
                last.then_inc(s_hw, 1)

            def hw_split(T):
                dve.wait_ge(s_hwh, T + 1)
                nc.vector.tensor_tensor(hwT_lo[:, T % 2], QK[T % 2][0][:, 0:P], hwT_hi[:, T % 2].bitcast(F32),
                                        ALU.subtract).then_inc(s_hwT, 1)

            def finish(T):
                dve.wait_ge(s_res, T + 1)
                dve.wait_ge(s_x1b, T + 1)
                nc.vector.tensor_tensor(X[:, T, :], D[T % TPH], X[:, T, :], ALU.add).then_inc(s_fin, 1)

            y_bias(0)
            y_split(0)
            y_bias(1)
            norm_stats(TPH)
            y_split(1)
            norm_stats(TPH + 1)
            norm_apply(TPH)
            norm_stats(TPH + 2)
            norm_apply(TPH + 1)
            norm_stats(TPH + 3)
            norm_apply(TPH + 2)
            scores(0)
            norm_apply(TPH + 3)
            weigh(0)
            scores(1)
            hw_split(0)
            y_bias(2)
            weigh(1)
            y_split(2)
            finish(0)
            y_bias(3)
            y_split(3)
            for T in range(1, TILES - 3):
                scores(T + 1)
                hw_split(T)
                weigh(T + 1)
                if T < TILES - 4:
                    finish(T)
                y_bias(T + 3)
                y_split(T + 3)
            a, b, c, d = range(TILES - 4, TILES)
            hw_split(b)
            finish(a)
            scores(c)
            weigh(c)
            scores(d)
            hw_split(c)
            weigh(d)
            finish(b)
            hw_split(d)
            finish(c)
            finish(d)

        @block.tensor
        def _(pe):
            def mm3(o, lh, ll, rh, rl, start, stop):
                nc.tensor.matmul(o, lh, rh, start=start, stop=False)
                nc.tensor.matmul(o, lh, rl, start=False, stop=False)
                return nc.tensor.matmul(o, ll, rh, start=False, stop=stop)

            def conv(T):
                if T == TPH:
                    pe.wait_ge(s_R, IC)
                if T == TPH + 2:
                    pe.wait_ge(s_lat, LC)
                for s in range(SPT):
                    for a in range(NWIN):
                        last = nc.tensor.matmul(conv_bank(T)[:, s * P:(s + 1) * P],
                                                XS[:, T % TPH * SPT + s, a:a + P], wconv[:, a],
                                                start=(a == 0), stop=(a == NWIN - 1))
                last.then_inc(s_conv, 1)

            def gate_rows(h):
                if h == 0:
                    pe.wait_ge(s_gate, 1)
                    pe.wait_ge(s_aT, 1)
                else:
                    pe.wait_ge(s_tf, TPH + 3)
                for p in range(PH):
                    nc.tensor.matmul(M[0], gate_hl[:, p], H_hi[:, p], start=(p == 0), stop=False)
                    last = nc.tensor.matmul(M[0], gate_hl[:, p], H_lo[:, p], start=False, stop=(p == PH - 1))
                last.then_inc(s_gT, 1)

            def gate_logits(h):
                pe.wait_ge(s_gTs, h + 1)
                if h == 0:
                    pe.wait_ge(s_exT, 1)
                else:
                    pe.wait_ge(s_tf, TILES)
                for t in range(TPH):
                    last = nc.tensor.transpose(M[1][:, t * 2 * NE:(t + 1) * 2 * NE],
                                               sbc[0:2 * NE, t * P:(t + 1) * P], ident[0:2 * NE, 0:2 * NE])
                last.then_inc(s_gp, 1)

            def up(i, part=None):
                h, c = divmod(i, IC)
                if h == 0:
                    pe.wait_ge(s_up, c + 1)
                if part is None:
                    part = slice(0, TOKH)
                if c < 2:
                    pe.wait_ge(s_H, TPH * h + part.stop // P)
                    pe.wait_ge(s_tf, TPH * h + c + 1)
                if i >= 2:
                    pe.wait_ge(s_R, i - 1)
                for p in range(PH):
                    last = mm3(U[i % 2][:, part], up_hi[:, c, p], up_lo[:, c, p], H_hi[:, p, part],
                               H_lo[:, p, part], p == 0, p == PH - 1)
                if part.stop == TOKH:
                    last.then_inc(s_upp, 1)

            def scale_rows(h):
                pe.wait_ge(s_diag, h + 1)
                pe.wait_ge(s_diagl, h + 1)
                nc.tensor.matmul(M[0], ones_r[:], diag_hi, start=True, stop=False)
                nc.tensor.matmul(M[0], ones_r[:], diag_lo, start=False, stop=True).then_inc(s_sbp, 1)

            def latent(n):
                h, c = divmod(n, LC)
                if c == 0:
                    pe.wait_ge(s_top, h + 1)
                else:
                    pe.wait_ge(s_sb, h + 1)
                if h == 0:
                    pe.wait_ge(s_fc, 1)
                for p in range(PH):
                    last = mm3(M[(n + 1) % LC], fc_hi[:, p, c * P:(c + 1) * P], fc_lo[:, p, c * P:(c + 1) * P],
                               H_hi[:, p], H_lo[:, p], p == 0, p == PH - 1)
                last.then_inc(s_latp, 1)

            def down(i):
                h, c = divmod(i, IC)
                pe.wait_ge(s_R, i + 1)
                if h == 0:
                    pe.wait_ge(s_dn, c + 1)
                for t in range(TPH):
                    if h and c == 0:
                        pe.wait_ge(s_x1, t + 1)
                    if h == 0 and c == 0:
                        pe.wait_ge(s_agg, 2)
                        pe.wait_ge(s_B1, 2)
                        pe.wait_ge(s_E2, LC)
                    ts = slice(t * P, (t + 1) * P)
                    last = mm3(D[t], R_hi[i % NR][:, ts], R_lo[i % NR][:, ts], dn_hi[:, c], dn_lo[:, c],
                               c == 0, c == IC - 1)
                    if c == IC - 1:
                        last.then_inc(s_ffn, 1)
                    elif t == TPH - 1:
                        last.then_inc(s_down, 1)

            def routed(h):
                pe.wait_ge(s_lat, LC * (h + 1))
                for t in range(TPH):
                    ts = slice(t * P, (t + 1) * P)
                    for c in range(LC):
                        mm3(D[t], lat_hi[:, c, ts], lat_lo[:, c, ts], ex_hi[:, c], ex_lo[:, c], False, False)

            def mix(T):
                if T == 0:
                    pe.wait_ge(s_BD, SPT)
                pe.wait_ge(s_x1, T + 1)
                if T < 2:
                    pe.wait_ge(s_lat, HALVES * LC)
                elif T < TPH:
                    pe.wait_ge(s_x1, TPH + T + 1)
                else:
                    pe.wait_ge(s_fin, T - TPH + 1)
                for p in range(PH):
                    last = nc.tensor.matmul(mix_bank(T)[:, p, :], X[:, T, p * P:(p + 1) * P], BD[:, T],
                                            start=True, stop=True)
                last.then_inc(s_yp, 1)

            def qk(T):
                ts = slice(T % TPH * P, (T % TPH + 1) * P)
                """q and one half of y @ A.T in the first bank, k and the other half in the second"""
                pe.wait_ge(s_Y, T + 1)
                if T == 0:
                    pe.wait_ge(s_wg, NG)
                if T >= 2:
                    pe.wait_ge(s_hwT, T - 1)
                for a in range(2):
                    for p in range(PH):
                        last = mm3(QK[T % 2][a][:, 0:QKW], H_hi[:, p, ts], H_lo[:, p, ts],
                                   qkT_hi[:, p, a], qkT_lo[:, p, a], p == 0, p == PH - 1)
                last.then_inc(s_qkp, 1)

            def dense(T):
                ts = slice(T % TPH * P, (T % TPH + 1) * P)
                if T < 2:
                    pe.wait_ge(s_x1, TPH + T + 1)
                for p in range(PH):
                    mm3(D[T % TPH], H_hi[:, p, ts], H_lo[:, p, ts], wT_hi[:, p], wT_lo[:, p], p == 0, False)

            def turn_hw(T):
                pe.wait_ge(s_hw, T + 1)
                nc.tensor.transpose(QK[T % 2][0][:, 0:P], hw[:], ident[:]).then_inc(s_hwp, 1)

            def combine(T):
                pe.wait_ge(s_hwT, T + 1)
                mm3(D[T % TPH], hwT_hi[:, T % 2], hwT_lo[:, T % 2], bT_hi[:], bT_lo[:], False, True)\
                    .then_inc(s_res, 1)

            def turn_expert():
                pe.wait_ge(ld_ex, 16)
                for mc in range(LC):
                    for lc in range(LC):
                        last = nc.tensor.transpose(M[1][:, mc * LAT + lc * P:mc * LAT + (lc + 1) * P],
                                                   exraw[:, lc, mc * P:(mc + 1) * P], ident[:])
                last.then_inc(s_exTp, 1)

            pe.wait_ge(s_ident, 2)
            pe.wait_ge(s_wcp, 1)
            for a in range(NWIN):
                for p in range(PH):
                    k0 = PH - 1 + PH * a - p
                    last = nc.tensor.transpose(M[1][:, a * P + p * C:a * P + (p + 1) * C],
                                               wc_pad[:, k0:k0 + PH, :].rearrange("p k c -> p (k c)"),
                                               ident[0:C, 0:C])
            last.then_inc(s_wcT, 1)
            pe.wait_ge(ld_c, 32)
            nc.tensor.transpose(M[0][:, 0:N], c_nat[:], ident[0:N, 0:N])
            nc.tensor.transpose(M[0][:, N:N + C], cw_nat[:], ident[0:C, 0:C]).then_inc(s_cTp, 1)
            pe.wait_ge(s_wconv, 1)
            pe.wait_ge(s_zero, 2)
            for t in range(2):
                pe.wait_ge(xs_v, t + 1)
                pe.wait_ge(xs_a, t + 1)
                conv(t)
            turn_expert()
            pe.wait_ge(s_ones, 2)
            pe.wait_ge(s_prod0s, 1)
            for i in range(2):
                bs = slice(i * BANK, (i + 1) * BANK)
                nc.tensor.matmul(D[i], ones_r[:], prod0_hi[:, bs], start=True, stop=False)
                nc.tensor.matmul(D[i], ones_r[:], prod0_lo[:, bs], start=False, stop=True).then_inc(s_B0p, 1)
            pe.wait_ge(ld_cond, 16 * 8)
            pe.wait_ge(s_cT, 1)
            nc.tensor.matmul(M[0][:, 0:N], W0[:], cT[:], start=True, stop=True).then_inc(s_c1p, 1)
            pe.wait_ge(xs_v, 3)
            pe.wait_ge(xs_a, 3)
            conv(2)
            conv(3)
            pe.wait_ge(s_c1, 1)
            nc.tensor.matmul(M[0][:, 0:N], W1[:], h1[:], start=True, stop=True).then_inc(s_c2p, 1)
            pe.wait_ge(s_exT, 1)
            pe.wait_ge(s_fc2, 1)
            pe.wait_ge(s_B0, 2)
            for lc in range(LC):
                for mc in range(LC):
                    ms = slice(lc * P, (lc + 1) * P)
                    last = mm3(D[lc], exT_hi[:, mc, ms], exT_lo[:, mc, ms], fc2_hi[:, mc], fc2_lo[:, mc],
                               mc == 0, mc == LC - 1)
                last.then_inc(s_E2p, 1)
                if lc == 0:
                    pe.wait_ge(s_c2, 1)
                    nc.tensor.matmul(M[0][0:N, 0:KE], h2[:], W2[:], start=True, stop=True).then_inc(s_lgp, 1)

            def turn_att():
                pe.wait_ge(s_att, 5)
                nc.tensor.transpose(M[0][0:KE, 0:N], att[:, 0, :], ident[0:N, 0:N]).then_inc(s_aTp, 1)

            def mixing():
                pe.wait_ge(s_aT, 1)
                pe.wait_ge(s_E2, LC)
                wf = wk[:].rearrange("k o i -> k (o i)")
                for b in range(2):
                    last = nc.tensor.matmul(D[b][0:N, :], attT[:], wf[:, b * BANK:(b + 1) * BANK],
                                            start=True, stop=True)
                last.then_inc(s_AGp, 1)

            def mixing_bias():
                pe.wait_ge(s_prod1s, 1)
                pe.wait_ge(s_tf, TPH)
                for i in range(2):
                    bs = slice(i * BANK, (i + 1) * BANK)
                    nc.tensor.matmul(D[2 + i], ones_r[0:KE, :], prod1_hi[:, bs], start=True, stop=False)
                    nc.tensor.matmul(D[2 + i], ones_r[0:KE, :], prod1_lo[:, bs], start=False, stop=True)\
                        .then_inc(s_B1p, 1)

            for h in range(HALVES):
                if h:
                    pe.wait_ge(xs_v, 4)
                    pe.wait_ge(xs_a, 4)
                    for t in range(TPH):
                        conv(TPH + t)
                for i in (h * IC, h * IC + 1):
                    up(i, slice(0, TOKH // 2))
                if h == 0:
                    turn_att()
                up(h * IC, slice(TOKH // 2, TOKH))
                if h == 0:
                    mixing()
                gate_rows(h)
                up(h * IC + 1, slice(TOKH // 2, TOKH))
                gate_logits(h)
                if h == 0:
                    mixing_bias()
                up(h * IC + 2)
                scale_rows(h)
                for n in range(LC):
                    latent(h * LC + n)
                for c in range(IC):
                    down(h * IC + c)
                    if c == 1:
                        routed(h)
                    if c + 3 < IC:
                        up(h * IC + c + 3)
                    if h and IC - 3 <= c < IC - 1:
                        mix(c - IC + 3)

            qk(0)
            qk(1)
            dense(0)
            mix(2)
            turn_hw(0)
            dense(1)
            combine(0)
            mix(3)
            for T in range(1, TILES - 3):
                qk(T + 1)
                turn_hw(T)
                dense(T + 1)
                if T < TILES - 4:
                    combine(T)
                mix(T + 3)
            a, b, c, d = range(TILES - 4, TILES)
            qk(c)
            turn_hw(b)
            combine(a)
            qk(d)
            dense(c)
            turn_hw(c)
            combine(b)
            dense(d)
            turn_hw(d)
            combine(c)
            combine(d)


_INS = ['x', 'cond_128', 'fside_S_0', 'L0_cond_weight', 'L0_cond_c_weight', 'L0_ffn_gate_w', 'L0_ffn_up_w',
        'L0_ffn_down_w', 'L0_ffn_fc1_w', 'L0_ffn_fc2_w', 'L0_ffn_expert_w', 'L0_ffn_ln_gamma', 'L0_ffn_ln_beta',
        'L1_cond_W0', 'L1_cond_b0', 'L1_cond_W1', 'L1_cond_b1', 'L1_cond_W2', 'L1_cond_b2', 'L1_cond_weight',
        'L1_cond_bias_k', 'L1_ffn_W', 'L1_ffn_b', 'L1_ffn_Wq', 'L1_ffn_Wk', 'L1_ffn_A', 'L1_ffn_Bm']
_OUTS = [((32, 32, 512), 'float32')]


def kernel(**inputs):
    import numpy as _np
    import concourse.bacc as _bacc
    from concourse import mybir as _mybir
    from concourse.bass_utils import run_bass_kernel_spmd as _run

    nc = _bacc.Bacc("TRN2", target_bir_lowering=False, num_devices=1, dynamic_dma_scratch_size=1024)
    arrays, args = {}, []
    for name in _INS:
        a = _np.ascontiguousarray(inputs[name])
        arrays[f"in_{name}_dram"] = a
        args.append(nc.dram_tensor(f"in_{name}_dram", a.shape, _mybir.dt.from_np(a.dtype), kind="ExternalInput").ap())
    for i, (shape, dtype) in enumerate(_OUTS):
        dt = _mybir.dt.from_np(_np.dtype(dtype))
        args.append(nc.dram_tensor(f"out_{i}_dram", shape, dt, kind="ExternalOutput").ap())
    bass_adaln_ffn(nc, *args)
    r = _run(nc, [arrays], core_ids=[0])
    got = tuple(r.results[0][f"out_{i}_dram"] for i in range(len(_OUTS)))
    return got[0]
```
